# Optimizing a Trainium2 kernel written in Bass

```python
import numpy as np
import jax
import jax.numpy as jnp

def _softmax(x, axis=-1):
    return jax.nn.softmax(x, axis=axis)

def _gelu(x):
    return jax.nn.gelu(x, approximate=True)

def _silu(x):
    return jax.nn.silu(x)

def _sigmoid(x):
    return jax.nn.sigmoid(x)

def _layernorm(x, axis=-1, eps=1e-05):
    m = jnp.mean(x, axis=axis, keepdims=True)
    v = jnp.var(x, axis=axis, keepdims=True)
    return (x - m) / jnp.sqrt(v + eps)

def _scatter_add(tgt, idx, src, axis=0):
    return tgt.at[idx].add(src)

def _segment_sum(src, seg, n):
    return jax.ops.segment_sum(src, seg, n)
kernel_name = 'mk_flamingo_gated_d1_seqx_r8_158b79'

def setup_inputs(seed: int=0):
    np.random.seed(seed)
    _w = jnp.asarray

    def _rec_inputs():
        import jax
        import jax.numpy as jnp
        _rk = jax.random.key(seed)
        x = -7.109e-05 + 0.9999 * jax.random.normal(jax.random.fold_in(_rk, 1), (4, 256, 256), jnp.float32)
        _lenS = 256 - jax.random.randint(jax.random.fold_in(_rk, 7), (4,), 0, max(1, 256 // 4) + 1, jnp.int32)
        _lenS2 = 256 - jax.random.randint(jax.random.fold_in(_rk, 8), (4,), 0, max(1, 256 // 4) + 1, jnp.int32)
        _ctx_512P = jax.random.normal(jax.random.fold_in(_rk, 11), (4, 16, 64), jnp.float32)
        _ctx_512c = jax.random.dirichlet(jax.random.fold_in(_rk, 511), 0.3 * jnp.ones((16,), jnp.float32), (4, 256))
        _ctx_512t = jnp.einsum('bsk,bkd->bsd', _ctx_512c, _ctx_512P)
        _ctx_512t = _ctx_512t * jax.lax.rsqrt(jnp.mean(jnp.square(_ctx_512t)) + 1e-12) * 0.953939
        ctx_512 = 2.81802e-05 + 1.00001 * (_ctx_512t + 0.3 * jax.random.normal(jax.random.fold_in(_rk, 611), (4, 256, 64), jnp.float32))
        _g = jax.random.normal(jax.random.fold_in(_rk, 9001), (2, 1), jnp.float32)
        _g = jnp.sign(_g) * jnp.maximum(jnp.abs(_g), 1.0) + (_g == 0) * 1.0
        g_xattn = _g[0]
        g_ffn = _g[1]
        return (x, ctx_512, g_xattn, g_ffn)
    x, ctx_512, g_xattn, g_ffn = _rec_inputs()

    def _L0_xattn_setup():
        import jax, jax.numpy as jnp
        import numpy as np
        EPS = 1e-06
        IMAGE_DIMS = 256
        key = jax.random.key(seed)
        k1, k2, k3 = jax.random.split(key, 3)
        B, I, J, D = (16, 256, 256, 64)
        p = jax.random.normal(k1, (B, I, J), dtype=jnp.float32)
        k_v = jax.random.normal(k2, (B, J, D), dtype=jnp.float32)
        W_k = jax.random.normal(k3, (D, D), dtype=jnp.float32) * (1.0 / np.sqrt(D))
        b_k = jnp.zeros((D,), dtype=jnp.float32)
        ln_gamma = jnp.ones((J,), dtype=jnp.float32)
        ln_beta = jnp.zeros((J,), dtype=jnp.float32)
        return {'p': p, 'k_v': k_v, 'W_k': W_k, 'b_k': b_k, 'ln_gamma': ln_gamma, 'ln_beta': ln_beta}
    _L0_xattn_all = _L0_xattn_setup()
    _L0_xattn_in = {k: v for k, v in _L0_xattn_all.items() if k in ('W_k', 'b_k', 'ln_gamma', 'ln_beta')}
    del _L0_xattn_all

    def _L0_ffn_setup():
        import jax, jax.numpy as jnp
        import numpy as np
        N_EXPERTS = 16
        TOP_K = 4
        N_GROUP = 4
        TOPK_GROUP = 2
        NORM_TOPK = True
        ROUTED_SCALE = 2.5
        H = 256
        F_MOE = 128
        F_SHARED = 256
        B, S = (2, 256)

        def _route(hidden, gate_weight, bias):
            T = hidden.shape[0]
            epg = N_EXPERTS // N_GROUP
            logits = hidden @ gate_weight.T
            scores = jax.nn.sigmoid(logits)
            scores_for_choice = scores + bias[None, :]
            grp = scores_for_choice.reshape(T, N_GROUP, epg)
            group_scores = jax.lax.top_k(grp, 2)[0].sum(-1)
            group_idx = jax.lax.top_k(group_scores, TOPK_GROUP)[1]
            group_mask = jax.nn.one_hot(group_idx, N_GROUP, dtype=jnp.bool_).any(1)
            score_mask = jnp.repeat(group_mask, epg, axis=-1)
            masked = jnp.where(score_mask, scores_for_choice, -jnp.inf)
            topk_idx = jax.lax.top_k(masked, TOP_K)[1]
            topk_weight = jnp.take_along_axis(scores, topk_idx, axis=1)
            return (topk_weight, topk_idx)

        def _swiglu(x, gw, uw, dw):
            return jax.nn.silu(x @ gw.T) * (x @ uw.T) @ dw.T
        key = jax.random.key(seed)
        ks = jax.random.split(key, 9)
        std = 0.02
        return {'hidden_states': jax.random.normal(ks[0], (B, S, H), jnp.float32), 'gate_weight': jax.random.normal(ks[1], (N_EXPERTS, H), jnp.float32) * std, 'e_score_correction_bias': jnp.zeros((N_EXPERTS,), jnp.float32), 'gate_w': jax.random.normal(ks[2], (N_EXPERTS, F_MOE, H), jnp.float32) * std, 'up_w': jax.random.normal(ks[3], (N_EXPERTS, F_MOE, H), jnp.float32) * std, 'down_w': jax.random.normal(ks[4], (N_EXPERTS, H, F_MOE), jnp.float32) * std, 'sh_gate_w': jax.random.normal(ks[5], (F_SHARED, H), jnp.float32) * std, 'sh_up_w': jax.random.normal(ks[6], (F_SHARED, H), jnp.float32) * std, 'sh_down_w': jax.random.normal(ks[7], (H, F_SHARED), jnp.float32) * std}
    _L0_ffn_all = _L0_ffn_setup()
    _L0_ffn_in = {k: v for k, v in _L0_ffn_all.items() if k in ('gate_weight', 'e_score_correction_bias', 'gate_w', 'up_w', 'down_w', 'sh_gate_w', 'sh_up_w', 'sh_down_w')}
    del _L0_ffn_all
    return {'x': x, 'ctx_512': ctx_512, 'g_xattn': g_xattn, 'g_ffn': g_ffn, 'L0_xattn_W_k': _L0_xattn_in['W_k'], 'L0_xattn_b_k': _L0_xattn_in['b_k'], 'L0_xattn_ln_gamma': _L0_xattn_in['ln_gamma'], 'L0_xattn_ln_beta': _L0_xattn_in['ln_beta'], 'L0_ffn_gate_weight': _L0_ffn_in['gate_weight'], 'L0_ffn_e_score_correction_bias': _L0_ffn_in['e_score_correction_bias'], 'L0_ffn_gate_w': _L0_ffn_in['gate_w'], 'L0_ffn_up_w': _L0_ffn_in['up_w'], 'L0_ffn_down_w': _L0_ffn_in['down_w'], 'L0_ffn_sh_gate_w': _L0_ffn_in['sh_gate_w'], 'L0_ffn_sh_up_w': _L0_ffn_in['sh_up_w'], 'L0_ffn_sh_down_w': _L0_ffn_in['sh_down_w']}

def reference(x, ctx_512, g_xattn, g_ffn, L0_xattn_W_k, L0_xattn_b_k, L0_xattn_ln_gamma, L0_xattn_ln_beta, L0_ffn_gate_weight, L0_ffn_e_score_correction_bias, L0_ffn_gate_w, L0_ffn_up_w, L0_ffn_down_w, L0_ffn_sh_gate_w, L0_ffn_sh_up_w, L0_ffn_sh_down_w):
    import jax
    import jax.numpy as jnp

    def _L0_xattn_ref(p, k_v, W_k, b_k, ln_gamma, ln_beta):
        import jax, jax.numpy as jnp
        import numpy as np
        EPS = 1e-06
        IMAGE_DIMS = 256
        kv = k_v @ W_k.T + b_k
        out = jnp.einsum('bij,bjd->bid', p, kv)
        scale = IMAGE_DIMS ** (-0.5)
        sim = jnp.einsum('bid,bjd->bij', out, kv) * scale
        mu = jnp.mean(sim, axis=-1, keepdims=True)
        var = jnp.var(sim, axis=-1, keepdims=True)
        sim = (sim - mu) * jax.lax.rsqrt(var + EPS) * ln_gamma + ln_beta
        attn = jax.nn.softmax(sim, axis=-1)
        return attn

    def _L0_ffn_ref(hidden_states, gate_weight, e_score_correction_bias, gate_w, up_w, down_w, sh_gate_w, sh_up_w, sh_down_w):
        import jax, jax.numpy as jnp
        import numpy as np
        N_EXPERTS = 16
        TOP_K = 4
        N_GROUP = 4
        TOPK_GROUP = 2
        NORM_TOPK = True
        ROUTED_SCALE = 2.5
        H = 256
        F_MOE = 128
        F_SHARED = 256
        B, S = (2, 256)

        def _route(hidden, gate_weight, bias):
            T = hidden.shape[0]
            epg = N_EXPERTS // N_GROUP
            logits = hidden @ gate_weight.T
            scores = jax.nn.sigmoid(logits)
            scores_for_choice = scores + bias[None, :]
            grp = scores_for_choice.reshape(T, N_GROUP, epg)
            group_scores = jax.lax.top_k(grp, 2)[0].sum(-1)
            group_idx = jax.lax.top_k(group_scores, TOPK_GROUP)[1]
            group_mask = jax.nn.one_hot(group_idx, N_GROUP, dtype=jnp.bool_).any(1)
            score_mask = jnp.repeat(group_mask, epg, axis=-1)
            masked = jnp.where(score_mask, scores_for_choice, -jnp.inf)
            topk_idx = jax.lax.top_k(masked, TOP_K)[1]
            topk_weight = jnp.take_along_axis(scores, topk_idx, axis=1)
            return (topk_weight, topk_idx)

        def _swiglu(x, gw, uw, dw):
            return jax.nn.silu(x @ gw.T) * (x @ uw.T) @ dw.T
        Bh, Sh, Hh = hidden_states.shape
        hidden = hidden_states.reshape(-1, Hh)
        topk_weight, topk_idx = _route(hidden, gate_weight, e_score_correction_bias)
        if NORM_TOPK:
            topk_weight = topk_weight / (topk_weight.sum(-1, keepdims=True) + 1e-20)
        topk_weight = topk_weight * ROUTED_SCALE
        one_hot = jax.nn.one_hot(topk_idx, N_EXPERTS, dtype=topk_weight.dtype)
        weight_matrix = (one_hot * topk_weight[..., None]).sum(1)
        g = jnp.einsum('th,nfh->ntf', hidden, gate_w)
        u = jnp.einsum('th,nfh->ntf', hidden, up_w)
        act = jax.nn.silu(g) * u
        routed = jnp.einsum('ntf,nhf,tn->th', act, down_w, weight_matrix)
        out = routed + _swiglu(hidden, sh_gate_w, sh_up_w, sh_down_w)
        return out.reshape(Bh, Sh, Hh)
    x = x + jnp.tanh(g_xattn[0]) * _L0_xattn_ref(_layernorm(x, axis=-1), ctx_512, L0_xattn_W_k, L0_xattn_b_k, L0_xattn_ln_gamma, L0_xattn_ln_beta)
    x = x + jnp.tanh(g_ffn[0]) * _L0_ffn_ref(_layernorm(x, axis=-1), L0_ffn_gate_weight, L0_ffn_e_score_correction_bias, L0_ffn_gate_w, L0_ffn_up_w, L0_ffn_down_w, L0_ffn_sh_gate_w, L0_ffn_sh_up_w, L0_ffn_sh_down_w)
    return x

_drawn_inputs = setup_inputs


def setup_inputs(seed=0):
    import zlib

    import numpy as np

    out = dict(_drawn_inputs(seed))
    spreads = {'L0_xattn_b_k': (0.0, 0.8),
     'L0_xattn_ln_gamma': (1.0, 0.6),
     'L0_xattn_ln_beta': (0.0, 0.8),
     'L0_ffn_e_score_correction_bias': (0.0, 0.627)}
    factors = {'ctx_512': 8.0,
     'L0_xattn_W_k': 8.0,
     'L0_ffn_gate_weight': 5.303,
     'L0_ffn_gate_w': 4.044,
     'L0_ffn_up_w': 3.998,
     'L0_ffn_down_w': 3.993,
     'L0_ffn_sh_gate_w': 3.598,
     'L0_ffn_sh_up_w': 3.561,
     'L0_ffn_sh_down_w': 3.559}
    for name, (base, spread) in spreads.items():
        noise = np.random.default_rng([zlib.crc32(name.encode()), seed]).standard_normal(out[name].shape)
        drawn = base * np.exp(spread * noise) if base else spread * noise
        out[name] = jnp.asarray(drawn.astype(out[name].dtype))
    for name, factor in factors.items():
        out[name] = (out[name] * factor).astype(out[name].dtype)
    return out
```

```python
from contextlib import ExitStack

import concourse.bass as bass
from concourse import mybir

F32 = mybir.dt.float32
F32R = mybir.dt.float32r
ALU = mybir.AluOpType
ACT = mybir.ActivationFunctionType
AX = mybir.AxisListType

P = 128
B, S, D = 4, 256, 256
CD = 64
E, FE = 16, 128
FS = 256
GROUPS, TOPK_GROUPS, TOPK = 4, 2, 4
ROUTED_SCALE = 2.5
NT = B * S // P
HALF = 4
HTOK = HALF * P
C = D // P
NSH = FS // P
NF = NSH + E
WCOL = 2 * C * P + D
GU = 2 * C * P
SIM_SCALE = float(D) ** -0.5
LN_EPS, SIM_EPS = 1e-5, 1e-6
PEN = float(2.0 ** 127)
OUT_OF_GROUP = -PEN / 2
V_GAMMA, V_BETA, V_BIAS, V_GATES = 0, S, 2 * S, 2 * S + E
VROW = 2 * S + E + 2


def build(nc, x, ctxw, vecs, route_w, w_packed, out):
    x_v = x.rearrange("(t p) d -> p t d", p=P)
    out_v = out.rearrange("(t p) d -> p t d", p=P)
    w_v = w_packed.rearrange("n p c -> p n c")
    weight_rows = nc.dram_tensor("weight_rows", (E, B * S), F32, kind="Internal").ap()

    with ExitStack() as ctx:
        def sb(name, shape, dt=F32):
            return ctx.enter_context(nc.sbuf_tensor(name, shape, dt))

        def sem(name):
            return ctx.enter_context(nc.semaphore(name))

        bank = [ctx.enter_context(nc.psum_tensor(f"bank{i}", [P, 512], F32)) for i in range(8)]
        gate_ps, up_ps = bank[0:2], bank[2:4]
        acc_ps = [bank[4:6], bank[6:8]]
        kv_ps, kvT_ps = bank[4], [bank[5], bank[3]]
        lnT_ps = [bank[0:2], bank[6:8]]
        qT_ps = [bank[2], bank[4]]
        sim_ps = [bank[0:2], bank[6:8]]
        hT_ps = [bank[2:4], bank[6:8]]
        logit_ps = bank[6]

        ident = sb("ident", [P, P])
        lower = sb("lower", [P, GROUPS, GROUPS])
        half_neg = sb("half_neg", [P, HALF])
        vec = sb("vec", [P, VROW])
        gamma, beta = vec[:, V_GAMMA:V_GAMMA + S], vec[:, V_BETA:V_BETA + S]
        gates = sb("gates", [P, 2])
        cw = sb("cw", [CD + 1, B * S + CD])
        gw = sb("gw", [P, C, E])
        gw_hi, gw_lo = sb("gw_hi", [P, C, E], F32R), sb("gw_lo", [P, C, E], F32R)
        kv = sb("kv", [P, NT, CD])
        kvT = sb("kvT", [CD, B * S])
        xs = sb("xs", [P, NT, D])
        ln = sb("ln", [P, NT, D])
        lnT = sb("lnT", [P, 2, C, HTOK])
        qT = sb("qT", [CD, 2, HTOK])
        centred = sb("centred", [P, NT, S])
        logit = sb("logit", [P, NT, S])
        prob = sb("prob", [P, NT, S])
        x1 = sb("x1", [P, NT, D])
        hid = sb("hid", [P, NT, D])
        hT_hi = sb("hT_hi", [P, 2, C, HTOK], F32R)
        hT_lo = sb("hT_lo", [P, 2, C, HTOK], F32R)
        stats = sb("stats", [P, 3, NT, 6])
        meanvar = sb("meanvar", [P, 3, NT, 2])
        var_eps = sb("var_eps", [P, 3, NT])
        rstd = sb("rstd", [P, 3, NT])
        sim_rstd = sb("sim_rstd", [P, NT])
        neg_max = sb("neg_max", [P, NT])
        exp_sum = sb("exp_sum", [P, NT])
        exp_rec = sb("exp_rec", [P, NT])
        attn_scale = sb("attn_scale", [P, NT])
        score = sb("score", [P, NT, E])
        choice = sb("choice", [P, NT, E])
        pairs = sb("pairs", [P, NT * GROUPS, 6])
        gscore = sb("gscore", [P, NT, GROUPS])
        beats = sb("beats", [P, NT, GROUPS * GROUPS])
        ties = sb("ties", [P, NT, GROUPS * GROUPS])
        rank = sb("rank", [P, NT * GROUPS])
        penalty = sb("penalty", [P, NT * GROUPS])
        masked = sb("masked", [P, NT, E])
        top8 = sb("top8", [P, NT, 8])
        replaced = sb("replaced", [P, NT, E])
        picked = sb("picked", [P, NT, E])
        pick_w = sb("pick_w", [P, NT, E])
        w_sum = sb("w_sum", [P, NT])
        w_rec = sb("w_rec", [P, NT])
        w_tok = sb("w_tok", [P, E, NT])
        w_blk = sb("w_blk", [P, E * NT])
        w_raw = sb("w_raw", [P, 2, WCOL])
        w_hi, w_lo = sb("w_hi", [P, 2, WCOL], F32R), sb("w_lo", [P, 2, WCOL], F32R)
        w_row = sb("w_row", [P, 2, 2, HTOK])
        silu_g = sb("silu_g", [P, 2, HTOK])
        weighted = sb("weighted", [P, 2, HTOK])
        act_f = sb("act_f", [P, 2, HTOK])
        act_hi, act_lo = sb("act_hi", [P, 2, HTOK], F32R), sb("act_lo", [P, 2, HTOK], F32R)
        ffnT = sb("ffnT", [P, 2, C, HTOK])
        res = sb("res", [P, NT, D])

        x_in = [sem(f"x_in{h}") for h in range(2)]
        ctxw_in, vec_in, gw_in = sem("ctxw_in"), sem("vec_in"), sem("gw_in")
        w_in = [sem(f"w_in{i}") for i in range(2)]
        row_in = [sem(f"row_in{i}") for i in range(2)]
        rows_out = sem("rows_out")
        out_done = sem("out_done")
        ident_ready, consts_ready = sem("ident_ready"), sem("consts_ready")
        gates_ready = sem("gates_ready")
        kv_done, kvT_done = sem("kv_done"), sem("kvT_done")
        kv_ready, kvT_ready = sem("kv_ready"), sem("kvT_ready")
        dve_order = sem("dve_order")
        var_ready, rstd_ready = sem("var_ready"), sem("rstd_ready")
        ln_ready = [sem(f"ln_ready{h}") for h in range(2)]
        lnT_done = [sem(f"lnT_done{h}") for h in range(2)]
        lnT0_ready = [sem(f"lnT0_ready{h}") for h in range(2)]
        lnT1_ready = [sem(f"lnT1_ready{h}") for h in range(2)]
        qT_done = [sem(f"qT_done{h}") for h in range(2)]
        qT_ready = [sem(f"qT_ready{h}") for h in range(2)]
        sim_done = [sem(f"sim_done{h}") for h in range(2)]
        sim_read = [sem(f"sim_read{h}") for h in range(2)]
        max_ready = [sem(f"max_ready{h}") for h in range(2)]
        exp_ready = [sem(f"exp_ready{h}") for h in range(2)]
        hid_ready = [sem(f"hid_ready{h}") for h in range(2)]
        hT_done = [sem(f"hT_done{h}") for h in range(2)]
        hThi_ready = [sem(f"hThi_ready{h}") for h in range(2)]
        hTlo_ready = [sem(f"hTlo_ready{h}") for h in range(2)]
        gwhi_ready, gwlo_ready = sem("gwhi_ready"), sem("gwlo_ready")
        logit_done, score_ready = sem("logit_done"), sem("score_ready")
        blk_ready = sem("blk_ready")
        hi_gu, hi_d = sem("hi_gu"), sem("hi_d")
        lo_gu, lo_d = sem("lo_gu"), sem("lo_d")
        gate_done, up_done = sem("gate_done"), sem("up_done")
        silu_done, weighted_done = sem("silu_done"), sem("weighted_done")
        act_done, acthi_done, actlo_done = sem("act_done"), sem("acthi_done"), sem("actlo_done")
        down_done = sem("down_done")
        ffn0_ready, ffn1_ready = sem("ffn0_ready"), sem("ffn1_ready")
        fin_done, res_ready = sem("fin_done"), sem("res_ready")

        block = ctx.enter_context(nc.Block())
        LOOPS = NF // 2 - 1

        def tiles(h):
            return range(HALF * h, HALF * h + HALF)

        @block.sync
        def _(sp):
            def load_slice(n, slot):
                sp.dma_start(w_raw[:, slot, :], w_v[:, n, :]).then_inc(w_in[slot], 16)

            def load_row(n, slot):
                row = weight_rows[bass.ds(n - NSH, 1), :].partition_broadcast(P)
                sp.dma_start(w_row[:, slot, :, :], row.rearrange("p o (h t) -> p (o h) t", h=2))\
                  .then_inc(row_in[slot], 16)

            for h in range(2):
                sp.dma_start(xs[:, HALF * h:HALF * h + HALF, :], x_v[:, HALF * h:HALF * h + HALF, :])\
                  .then_inc(x_in[h], 16)
            load_slice(0, 0)
            load_slice(1, 1)
            for n in range(2, 4):
                sp.wait_ge(lo_d, n - 1)
                load_slice(n, n % 2)
            sp.wait_ge(blk_ready, 1)
            rows = weight_rows.rearrange("(c n) (t q k) -> q (n t) c k", c=4, q=4, k=32)
            for q in range(4):
                sp.dma_start(rows[q], w_blk[32 * q:32 * q + 32, :].rearrange("p (c k) -> p c k", c=4))\
                  .then_inc(rows_out, 16)
            sp.wait_ge(rows_out, 64)
            for n in range(2, 4):
                load_row(n, n % 2)
            with sp.Fori(1, LOOPS) as j:
                for s in range(2):
                    sp.wait_ge(lo_d, 2 * j + (s + 1))
                    load_slice(2 * j + (2 + s), s)
                    sp.wait_ge(weighted_done, 4 * j - (2 - 2 * s))
                    load_row(2 * j + (2 + s), s)
            for h in range(2):
                for b in range(2):
                    t = HALF * h + 2 * b
                    sp.wait_ge(res_ready, 2 * h + b + 1)
                    sp.dma_start(out_v[:, t:t + 2, :], res[:, t:t + 2, :]).then_inc(out_done, 16)
            sp.wait_ge(out_done, 64)

        @block.gpsimd
        def _(pool):
            nc.gpsimd.memset(ident[:], 0.0).then_inc(ident_ready, 1)
            pool.wait_ge(ident_ready, 1)
            nc.gpsimd.affine_select(out=ident[:], in_=ident[:], compare_op=ALU.not_equal, fill=1.0,
                                    base=0, pattern=[[-1, P]], channel_multiplier=1).then_inc(ident_ready, 1)
            nc.gpsimd.memset(half_neg[:], -0.5).then_inc(consts_ready, 1)
            nc.gpsimd.memset(lower[:], 0.0).then_inc(consts_ready, 1)
            pool.wait_ge(consts_ready, 2)
            for g in range(1, GROUPS):
                nc.gpsimd.memset(lower[:, g, 0:g], 1.0).then_inc(consts_ready, 1)

            def root(layer, h):
                pool.wait_ge(var_ready, root.n + 1)
                t = slice(HALF * h, HALF * h + HALF)
                nc.gpsimd.tensor_tensor(rstd[:, layer, t], var_eps[:, layer, t], half_neg[:], ALU.pow)\
                  .then_inc(rstd_ready, 1)
                root.n += 1
            root.n = 0

            def low_parts(n, slot):
                for part, cols, hi, done in ((0, slice(0, GU), hi_gu, lo_gu), (1, slice(GU, WCOL), hi_d, lo_d)):
                    pool.wait_ge(hi, n + 1)
                    nc.gpsimd.tensor_tensor(w_lo[:, slot, cols], w_raw[:, slot, cols],
                                            w_hi[:, slot, cols].bitcast(F32), ALU.subtract).then_inc(done, 1)

            root(0, 0)
            root(0, 1)
            pool.wait_ge(gwhi_ready, 1)
            nc.gpsimd.tensor_tensor(gw_lo[:], gw[:], gw_hi[:].bitcast(F32), ALU.subtract).then_inc(gwlo_ready, 1)
            low_parts(0, 0)
            root(1, 0)
            root(1, 1)
            low_parts(1, 1)
            root(2, 0)
            root(2, 1)
            low_parts(2, 0)
            with pool.Fori(1, LOOPS) as j:
                low_parts(2 * j + 1, 1)
                low_parts(2 * j + 2, 0)
            low_parts(NF - 1, 1)

        @block.scalar
        def _(act):
            act.dma_start(cw[:], ctxw).then_inc(ctxw_in, 16)
            act.dma_start(vec[:], vecs.partition_broadcast(P).rearrange("p o v -> p (o v)")).then_inc(vec_in, 16)
            act.dma_start(gw[:], route_w.rearrange("(c p) e -> p c e", p=P)).then_inc(gw_in, 16)

            def high_part(n, slot, cols, done):
                nc.scalar.copy(w_hi[:, slot, cols], w_raw[:, slot, cols]).then_inc(done, 1)

            def high_gu(n, slot, landed, free=None):
                act.wait_ge(w_in[slot], landed)
                if free is not None:
                    act.wait_ge(up_done, free)
                high_part(n, slot, slice(0, GU), hi_gu)

            def high_d(n, slot, free=None):
                if free is not None:
                    act.wait_ge(down_done, free)
                high_part(n, slot, slice(GU, WCOL), hi_d)

            act.wait_ge(vec_in, 16)
            nc.scalar.activation(gates[:], vec[:, V_GATES:V_GATES + 2], ACT.Tanh).then_inc(gates_ready, 1)
            act.wait_ge(gw_in, 16)
            nc.scalar.copy(gw_hi[:], gw[:]).then_inc(gwhi_ready, 1)
            for i in range(2):
                act.wait_ge(kvT_done, i + 1)
                nc.scalar.copy(kvT[:, i * 512:(i + 1) * 512], kvT_ps[i][0:CD, :]).then_inc(kvT_ready, 1)

            def ln_copy(h):
                act.wait_ge(lnT_done[h], 1)
                nc.scalar.copy(lnT[:, h, 0, :], lnT_ps[h][0][:, :]).then_inc(lnT0_ready[h], 1)

            def q_copy(h):
                act.wait_ge(qT_done[h], 1)
                nc.scalar.copy(qT[:, h, :], qT_ps[h][0:CD, :]).then_inc(qT_ready[h], 1)

            def softmax_exp(h):
                for i, t in enumerate(tiles(h)):
                    act.wait_ge(max_ready[h], i // 2 + 1)
                    nc.scalar.activation(prob[:, t, :], logit[:, t, :], ACT.Exp, bias=neg_max[:, t:t + 1],
                                         accum_out=exp_sum[:, t:t + 1]).then_inc(exp_ready[h], 1)

            def hidden_high(h):
                act.wait_ge(hT_done[h], 1)
                for c in range(C):
                    nc.scalar.copy(hT_hi[:, h, c, :], hT_ps[h][c][:, :]).then_inc(hThi_ready[h], 1)

            def silu(k, par, first=False):
                act.wait_ge(gate_done, k + 1)
                if not first:
                    act.wait_ge(act_done, k - 1)
                nc.scalar.activation(silu_g[:, par, :], gate_ps[par][:, :], ACT.Silu).then_inc(silu_done, 1)

            def act_high(k, par, first=False):
                act.wait_ge(act_done, k + 1)
                if not first:
                    act.wait_ge(down_done, k - 1)
                nc.scalar.copy(act_hi[:, par, :], act_f[:, par, :]).then_inc(acthi_done, 1)

            ln_copy(0)
            high_gu(0, 0, 16)
            q_copy(0)
            high_d(0, 0)
            ln_copy(1)
            high_gu(1, 1, 16)
            q_copy(1)
            high_d(1, 1)
            softmax_exp(0)
            hidden_high(0)
            softmax_exp(1)
            silu(0, 0, True)
            act_high(0, 0, True)
            silu(1, 1, True)
            hidden_high(1)
            act_high(1, 1, True)
            act.wait_ge(logit_done, 1)
            nc.scalar.activation(score[:, :, :], logit_ps[:, 0:NT * E].rearrange("p (t e) -> p t e", e=E),
                                 ACT.Sigmoid).then_inc(score_ready, 1)
            silu(2, 0)
            act_high(2, 0)
            silu(3, 1)
            high_gu(2, 0, 32, 3)
            act_high(3, 1)
            high_d(2, 0, 3)

            def pair(j, last):
                for s in range(4):
                    k = 4 * j + s
                    silu(k, s % 2)
                    split = s % 2 == 0 and not (last and s == 2)
                    m = 2 * j + (s // 2 + 1)
                    slot = 1 - s // 2
                    if split:
                        high_gu(m, slot, 16 * j + (16 if s == 0 else 32), 2 * m - 2)
                    act_high(k, s % 2)
                    if split:
                        high_d(m, slot, 2 * m - 2)

            with act.Fori(1, LOOPS) as j:
                pair(j, False)
            pair(LOOPS, True)
            for h in range(2):
                act.wait_ge(down_done, 2 * NF - 1 + h)
                nc.scalar.copy(ffnT[:, h, 0, :], acc_ps[h][0][:, :]).then_inc(ffn0_ready, 1)

        @block.vector
        def _(dve):
            order = [0]

            def link(ins):
                order[0] += 1
                ins.then_inc(dve_order, 1)
                dve.wait_ge(dve_order, order[0])

            def mean_var(layer, h, source, waits, scale2, eps):
                for i, t in enumerate(tiles(h)):
                    waits(i)
                    ins = nc.vector.bn_stats(stats[:, layer, t, :], source(t))
                    if i == HALF - 1:
                        link(ins)
                for i, t in enumerate(tiles(h)):
                    ins = nc.vector.bn_aggr(meanvar[:, layer, t, :], stats[:, layer, t, :])
                link(ins)
                ts = slice(HALF * h, HALF * h + HALF)
                nc.vector.tensor_scalar(var_eps[:, layer, ts], meanvar[:, layer, ts, 1], scale2, eps,
                                        ALU.mult, ALU.add).then_inc(var_ready, 1)

            def normalise(layer, h, n_root, source, dst, ready):
                dve.wait_ge(rstd_ready, n_root)
                for t in tiles(h):
                    nc.vector.tensor_scalar(dst[:, t, :], source[:, t, :], meanvar[:, layer, t, 0:1],
                                            rstd[:, layer, t:t + 1], ALU.subtract, ALU.mult).then_inc(ready, 1)

            def ln_copy(h):
                dve.wait_ge(lnT_done[h], 1)
                nc.vector.tensor_copy(lnT[:, h, 1, :], lnT_ps[h][1][:, :]).then_inc(lnT1_ready[h], 1)

            def sim_of(h, t):
                return sim_ps[h][(t - HALF * h) // 2][:, (t % 2) * S:(t % 2 + 1) * S]

            def sim_stats(h):
                mean_var(1, h, lambda t: sim_of(h, t), lambda i: dve.wait_ge(sim_done[h], i // 2 + 1),
                         SIM_SCALE ** 2, SIM_EPS)

            def sim_centre(h):
                for t in tiles(h):
                    nc.vector.scalar_tensor_tensor(centred[:, t, :], sim_of(h, t), meanvar[:, 1, t, 0:1], gamma,
                                                   ALU.subtract, ALU.mult).then_inc(sim_read[h], 1)

            def sim_logits(h, n_root):
                ts = slice(HALF * h, HALF * h + HALF)
                dve.wait_ge(rstd_ready, n_root)
                link(nc.vector.tensor_scalar(sim_rstd[:, ts], rstd[:, 1, ts], SIM_SCALE, None, ALU.mult))
                dve.wait_ge(sim_read[h], HALF)
                for p in range(2):
                    t0 = HALF * h + 2 * p
                    for t in (t0, t0 + 1):
                        ins = nc.vector.scalar_tensor_tensor(logit[:, t, :], centred[:, t, :], sim_rstd[:, t:t + 1],
                                                             beta, ALU.mult, ALU.add)
                    link(ins)
                    nc.vector.tensor_reduce(neg_max[:, t0:t0 + 2], logit[:, t0:t0 + 2, :], AX.X, ALU.max,
                                            negate=True).then_inc(max_ready[h], 1)

            def residual(h):
                for p in range(2):
                    t0 = HALF * h + 2 * p
                    dve.wait_ge(exp_ready[h], 2 * p + 2)
                    link(nc.vector.reciprocal(exp_rec[:, t0:t0 + 2], exp_sum[:, t0:t0 + 2]))
                    link(nc.vector.tensor_scalar(attn_scale[:, t0:t0 + 2], exp_rec[:, t0:t0 + 2], gates[:, 0:1],
                                                 None, ALU.mult))
                    for t in (t0, t0 + 1):
                        ins = nc.vector.scalar_tensor_tensor(x1[:, t, :], prob[:, t, :], attn_scale[:, t:t + 1],
                                                             xs[:, t, :], ALU.mult, ALU.add)
                link(ins)
                mean_var(2, h, lambda t: x1[:, t, :], lambda i: None, 1.0, LN_EPS)

            def hidden_low(h):
                for c in range(C):
                    dve.wait_ge(hThi_ready[h], c + 1)
                    nc.vector.tensor_tensor(hT_lo[:, h, c, :], hT_ps[h][c][:, :], hT_hi[:, h, c, :].bitcast(F32),
                                            ALU.subtract).then_inc(hTlo_ready[h], 1)

            def activate(k, par, routed=False, slot=None, half=None, row=None, first=False):
                gated = silu_g
                dve.wait_ge(silu_done, k + 1)
                if routed:
                    dve.wait_ge(row_in[slot], row)
                    nc.vector.tensor_tensor(weighted[:, par, :], silu_g[:, par, :], w_row[:, slot, half, :],
                                            ALU.mult).then_inc(weighted_done, 1)
                    dve.wait_ge(weighted_done, k - 3)
                    gated = weighted
                dve.wait_ge(up_done, k + 1)
                if not first:
                    dve.wait_ge(actlo_done, k - 1)
                nc.vector.tensor_tensor(act_f[:, par, :], up_ps[par][:, :], gated[:, par, :], ALU.mult)\
                  .then_inc(act_done, 1)

            def act_low(k, par, first=False):
                dve.wait_ge(acthi_done, k + 1)
                if not first:
                    dve.wait_ge(down_done, k - 1)
                nc.vector.tensor_tensor(act_lo[:, par, :], act_f[:, par, :], act_hi[:, par, :].bitcast(F32),
                                        ALU.subtract).then_inc(actlo_done, 1)

            def router():
                def grid(a, g):
                    return a.rearrange("p t (g h) -> p t g h", g=g)

                dve.wait_ge(score_ready, 1)
                bias = vec[:, V_BIAS:V_BIAS + E].unsqueeze(1).to_broadcast([P, NT, E])
                link(nc.vector.tensor_tensor(choice[:], score[:], bias, ALU.add))
                member = choice[:].rearrange("p t (g m) -> p (t g) m", g=GROUPS)
                nc.vector.tensor_tensor(pairs[:, :, 0:3], member[:, :, 0:3], member[:, :, 1:4], ALU.add)
                nc.vector.tensor_tensor(pairs[:, :, 3:5], member[:, :, 0:2], member[:, :, 2:4], ALU.add)
                link(nc.vector.tensor_tensor(pairs[:, :, 5:6], member[:, :, 0:1], member[:, :, 3:4], ALU.add))
                link(nc.vector.tensor_reduce(gscore[:].rearrange("p t g -> p (t g)"), pairs[:], AX.X, ALU.max))
                other = gscore[:].unsqueeze(2).to_broadcast([P, NT, GROUPS, GROUPS])
                own = gscore[:].unsqueeze(3).to_broadcast([P, NT, GROUPS, GROUPS])
                nc.vector.tensor_tensor(grid(beats[:], GROUPS), other, own, ALU.is_gt)
                link(nc.vector.tensor_tensor(grid(ties[:], GROUPS), other, own, ALU.is_equal))
                before = lower[:].rearrange("p g h -> p (g h)").unsqueeze(1).to_broadcast([P, NT, GROUPS * GROUPS])
                link(nc.vector.tensor_tensor(ties[:], ties[:], before, ALU.mult))
                link(nc.vector.tensor_tensor(beats[:], beats[:], ties[:], ALU.add))
                link(nc.vector.tensor_reduce(rank[:], beats[:].rearrange("p t (g h) -> p (t g) h", g=GROUPS),
                                             AX.X, ALU.add))
                link(nc.vector.tensor_scalar(penalty[:], rank[:], TOPK_GROUPS - 0.5, -PEN, ALU.subtract, ALU.mult))
                link(nc.vector.tensor_tensor(masked[:].rearrange("p t (g m) -> p (t g) m", g=GROUPS), member,
                                             penalty[:].unsqueeze(2).to_broadcast([P, NT * GROUPS, GROUPS]), ALU.min))
                for t in range(NT):
                    ins = nc.vector.max(top8[:, t, :], masked[:, t, :])
                link(ins)
                link(nc.vector.memset(top8[:, :, TOPK:8], OUT_OF_GROUP))
                for t in range(NT):
                    ins = nc.vector.match_replace(replaced[:, t, :], top8[:, t, :], masked[:, t, :], OUT_OF_GROUP)
                link(ins)
                link(nc.vector.tensor_tensor(picked[:], masked[:], replaced[:], ALU.not_equal))
                link(nc.vector.tensor_tensor(pick_w[:], picked[:], score[:], ALU.mult))
                link(nc.vector.tensor_reduce(w_sum[:], pick_w[:], AX.X, ALU.add))
                link(nc.vector.tensor_scalar(w_sum[:], w_sum[:], 1e-20, None, ALU.add))
                link(nc.vector.reciprocal(w_rec[:], w_sum[:]))
                link(nc.vector.tensor_scalar(w_rec[:], w_rec[:], ROUTED_SCALE, None, ALU.mult))
                link(nc.vector.tensor_tensor(w_tok[:].rearrange("p e t -> p t e"), pick_w[:],
                                             w_rec[:].unsqueeze(2).to_broadcast([P, NT, E]), ALU.mult))
                nc.vector.transpose(w_blk[:], w_tok[:].rearrange("p e t -> p (e t)")).then_inc(blk_ready, 1)

            mean_var(0, 0, lambda t: xs[:, t, :], lambda i: dve.wait_ge(x_in[0], 16), 1.0, LN_EPS)
            mean_var(0, 1, lambda t: xs[:, t, :], lambda i: dve.wait_ge(x_in[1], 16), 1.0, LN_EPS)
            normalise(0, 0, 1, xs, ln, ln_ready[0])
            dve.wait_ge(kv_done, 1)
            nc.vector.tensor_copy(kv[:].rearrange("p t d -> p (t d)"), kv_ps[:, :]).then_inc(kv_ready, 1)
            normalise(0, 1, 2, xs, ln, ln_ready[1])
            ln_copy(0)
            ln_copy(1)
            dve.wait_ge(vec_in, 16)
            sim_stats(0)
            sim_centre(0)
            sim_stats(1)
            sim_logits(0, 3)
            sim_centre(1)
            dve.wait_ge(gates_ready, 1)
            residual(0)
            sim_logits(1, 4)
            normalise(2, 0, 5, x1, hid, hid_ready[0])
            hidden_low(0)
            residual(1)
            activate(0, 0, first=True)
            normalise(2, 1, 6, x1, hid, hid_ready[1])
            act_low(0, 0, True)
            activate(1, 1, first=True)
            hidden_low(1)
            act_low(1, 1, True)
            dve.wait_ge(consts_ready, 2 + GROUPS - 1)
            router()
            activate(2, 0)
            act_low(2, 0)
            activate(3, 1)
            act_low(3, 1)

            def pair(j):
                for s in range(4):
                    k = 4 * j + s
                    activate(k, s % 2, True, s // 2, s % 2, 16 * j)
                    act_low(k, s % 2)

            with dve.Fori(1, LOOPS) as j:
                pair(j)
            pair(LOOPS)
            for h in range(2):
                dve.wait_ge(down_done, 2 * NF - 1 + h)
                nc.vector.tensor_copy(ffnT[:, h, 1, :], acc_ps[h][1][:, :]).then_inc(ffn1_ready, 1)
            fin_ps = [gate_ps, up_ps]
            for h in range(2):
                for b in range(2):
                    t = HALF * h + 2 * b
                    dve.wait_ge(fin_done, 2 * h + b + 1)
                    nc.vector.scalar_tensor_tensor(res[:, t:t + 2, :].rearrange("p t d -> p (t d)"),
                                                   fin_ps[h][b][:, :], gates[:, 1:2],
                                                   x1[:, t:t + 2, :].rearrange("p t d -> p (t d)"),
                                                   ALU.mult, ALU.add).then_inc(res_ready, 1)

        @block.tensor
        def _(pe):
            wk = cw[:, B * S:B * S + CD]
            pe.wait_ge(ctxw_in, 16)
            for i in range(2):
                nc.tensor.matmul(kvT_ps[i][0:CD, :], wk, cw[:, i * 512:(i + 1) * 512], start=True, stop=True)\
                  .then_inc(kvT_done, 1)
            for t in range(NT):
                last = nc.tensor.matmul(kv_ps[:, t * CD:(t + 1) * CD], cw[:, t * P:(t + 1) * P], wk,
                                        start=True, stop=True)
            last.then_inc(kv_done, 1)
            pe.wait_ge(ident_ready, 2)

            def transposes(h, dst, source, ready, done):
                for i, t in enumerate(tiles(h)):
                    pe.wait_ge(ready, i + 1)
                    for c in range(C):
                        last = nc.tensor.transpose(dst[h][c][:, i * P:(i + 1) * P],
                                                   source[:, t, c * P:(c + 1) * P], ident[:])
                last.then_inc(done, 1)

            def query(h):
                pe.wait_ge(lnT0_ready[h], 1)
                pe.wait_ge(lnT1_ready[h], 1)
                pe.wait_ge(kv_ready, 1)
                for b in range(2):
                    cols = slice(b * S, (b + 1) * S)
                    for c in range(C):
                        last = nc.tensor.matmul(qT_ps[h][0:CD, cols], kv[:, HALF * h + 2 * b + c, :],
                                                lnT[:, h, c, cols], start=(c == 0), stop=(c == C - 1))
                last.then_inc(qT_done[h], 1)

            def similarity(h):
                pe.wait_ge(qT_ready[h], 1)
                pe.wait_ge(kvT_ready, h + 1)
                for b in range(2):
                    for i in range(2):
                        last = nc.tensor.matmul(sim_ps[h][b][:, i * S:(i + 1) * S],
                                                qT[:, h, (2 * b + i) * P:(2 * b + i + 1) * P],
                                                kvT[:, (2 * h + b) * S:(2 * h + b + 1) * S], start=True, stop=True)
                    last.then_inc(sim_done[h], 1)

            def product(dst, w0, halves, slot, start, stop, skip=True):
                n = len(halves)
                for i, (m_hi, m_lo) in enumerate(halves):
                    cols = slice(w0 + i * P, w0 + (i + 1) * P)
                    for r, (w, m) in enumerate(((w_hi, m_hi), (w_hi, m_lo), (w_lo, m_hi))):
                        last = nc.tensor.matmul(dst, w[:, slot, cols], m, start=start and i == r == 0,
                                                stop=stop and i == n - 1 and r == 2, skip_group_check=skip)
                return last

            def gate_up(k, par, slot, half, n, first=False):
                pe.wait_ge(hi_gu, n + 1)
                pe.wait_ge(lo_gu, n + 1)
                moving = [(hT_hi[:, half, c, :], hT_lo[:, half, c, :]) for c in range(C)]
                if not first:
                    pe.wait_ge(silu_done, k - 1)
                product(gate_ps[par][:, :], 0, moving, slot, True, True).then_inc(gate_done, 1)
                if not first:
                    pe.wait_ge(act_done, k - 1)
                product(up_ps[par][:, :], C * P, moving, slot, True, True).then_inc(up_done, 1)

            def down(k, par, slot, half, n, start=False):
                pe.wait_ge(hi_d, n + 1)
                pe.wait_ge(lo_d, n + 1)
                pe.wait_ge(acthi_done, k + 1)
                for i, (w, m, ready) in enumerate(((w_hi, act_hi, None), (w_lo, act_hi, None), (w_hi, act_lo, actlo_done))):
                    if ready is not None:
                        pe.wait_ge(ready, k + 1)
                    for c in range(C):
                        cols = slice(GU + c * P, GU + (c + 1) * P)
                        last = nc.tensor.matmul(acc_ps[half][c][:, :], w[:, slot, cols], m[:, par, :],
                                                start=start and i == 0, stop=i == 2, skip_group_check=True)
                last.then_inc(down_done, 1)

            transposes(0, lnT_ps, ln, ln_ready[0], lnT_done[0])
            transposes(1, lnT_ps, ln, ln_ready[1], lnT_done[1])
            query(0)
            similarity(0)
            query(1)
            similarity(1)
            pe.wait_ge(kvT_ready, 2)
            transposes(0, hT_ps, hid, hid_ready[0], hT_done[0])
            pe.wait_ge(sim_read[0], HALF)
            pe.wait_ge(hTlo_ready[0], C)
            gate_up(0, 0, 0, 0, 0, True)
            gate_up(1, 1, 1, 0, 1, True)
            down(0, 0, 0, 0, 0, True)
            pe.wait_ge(sim_read[1], HALF)
            transposes(1, hT_ps, hid, hid_ready[1], hT_done[1])
            down(1, 1, 1, 0, 1)
            pe.wait_ge(hTlo_ready[1], C)
            pe.wait_ge(gwlo_ready, 1)
            for t in range(NT):
                h, cols = t // HALF, slice(t % HALF * P, (t % HALF + 1) * P)
                parts = [(m, w, c) for c in range(C) for m in (hT_hi, hT_lo) for w in (gw_hi, gw_lo)]
                for i, (m, w, c) in enumerate(parts):
                    last = nc.tensor.matmul(logit_ps[:, t * E:(t + 1) * E], m[:, h, c, cols], w[:, c, :],
                                            start=(i == 0), stop=(i == len(parts) - 1))
            last.then_inc(logit_done, 1)
            gate_up(2, 0, 0, 1, 0)
            gate_up(3, 1, 1, 1, 1)
            pe.wait_ge(score_ready, 1)
            down(2, 0, 0, 1, 0, True)

            def pair(j, first=False):
                for s in range(4):
                    k, n = 4 * j + s, 2 * j + s // 2
                    gate_up(k, s % 2, s // 2, s % 2, n)
                    p = s - 1
                    if p < 0:
                        down(k - 1, 1, 1, 1, n - 1)
                    else:
                        down(k - 1, p % 2, p // 2, p % 2, 2 * j + p // 2)

            with pe.Fori(1, LOOPS) as j:
                pair(j)
            pair(LOOPS)
            down(2 * NF - 1, 1, 1, 1, NF - 1)
            fin_ps = [gate_ps, up_ps]
            pe.wait_ge(silu_done, 2 * NF)
            pe.wait_ge(act_done, 2 * NF)
            for h in range(2):
                pe.wait_ge(ffn0_ready, h + 1)
                pe.wait_ge(ffn1_ready, h + 1)
                for b in range(2):
                    for i in range(2):
                        for c in range(C):
                            tok = slice((2 * b + i) * P, (2 * b + i + 1) * P)
                            last = nc.tensor.transpose(fin_ps[h][b][:, i * D + c * P:i * D + (c + 1) * P],
                                                       ffnT[:, h, c, tok], ident[:])
                    last.then_inc(fin_done, 1)


def kernel(x, ctx_512, g_xattn, g_ffn, L0_xattn_W_k, L0_xattn_b_k, L0_xattn_ln_gamma, L0_xattn_ln_beta,
           L0_ffn_gate_weight, L0_ffn_e_score_correction_bias, L0_ffn_gate_w, L0_ffn_up_w, L0_ffn_down_w,
           L0_ffn_sh_gate_w, L0_ffn_sh_up_w, L0_ffn_sh_down_w):
    import numpy as np
    import concourse.bacc as bacc
    from concourse.bass_utils import run_bass_kernel_spmd as run

    def arr(a):
        return np.asarray(a)

    def slices(gate, up, down):
        n = gate.shape[0]
        parts = [w.transpose(0, 2, 1).reshape(n, C, P, P).transpose(0, 2, 1, 3).reshape(n, P, C * P)
                 for w in (gate, up)]
        return np.concatenate(parts + [down.transpose(0, 2, 1)], axis=2)

    tokens = B * S
    ctxT = arr(ctx_512).reshape(tokens, CD).T
    ones = np.ones((1, tokens), np.float32)
    wk = np.concatenate([arr(L0_xattn_W_k).T, arr(L0_xattn_b_k).reshape(1, CD)], axis=0)
    sh = slices(arr(L0_ffn_sh_gate_w).reshape(NSH, P, D), arr(L0_ffn_sh_up_w).reshape(NSH, P, D),
                arr(L0_ffn_sh_down_w).reshape(D, NSH, P).transpose(1, 0, 2))
    arrays = {
        "x_in": arr(x).reshape(tokens, D),
        "ctxw_in": np.concatenate([np.concatenate([ctxT, ones], axis=0), wk], axis=1),
        "vecs_in": np.concatenate([arr(a).reshape(-1) for a in (
            L0_xattn_ln_gamma, L0_xattn_ln_beta, L0_ffn_e_score_correction_bias, g_xattn, g_ffn)]).reshape(1, -1),
        "route_in": arr(L0_ffn_gate_weight).T,
        "w_in": np.concatenate([sh, slices(arr(L0_ffn_gate_w), arr(L0_ffn_up_w), arr(L0_ffn_down_w))], axis=0),
    }
    arrays = {k: np.ascontiguousarray(v) for k, v in arrays.items()}
    nc = bacc.Bacc("TRN2", target_bir_lowering=False, num_devices=1)
    args = [nc.dram_tensor(k, v.shape, F32, kind="ExternalInput").ap() for k, v in arrays.items()]
    out = nc.dram_tensor("out", (tokens, D), F32, kind="ExternalOutput").ap()
    build(nc, *args, out)
    r = run(nc, [arrays], core_ids=[0])
    return r.results[0]["out"].reshape(B, S, D)
```

```python
from contextlib import ExitStack

import concourse.bass as bass
from concourse import mybir

F32 = mybir.dt.float32
F32R = mybir.dt.float32r
ALU = mybir.AluOpType
ACT = mybir.ActivationFunctionType
AX = mybir.AxisListType

P = 128
B, S, D = 4, 256, 256
CD = 64
E, FE = 16, 128
FS = 256
GROUPS, TOPK_GROUPS, TOPK = 4, 2, 4
ROUTED_SCALE = 2.5
NT = B * S // P
HALF = 4
HTOK = HALF * P
C = D // P
NSH = FS // P
NF = NSH + E
WCOL = 2 * C * P + D
GU = 2 * C * P
SIM_SCALE = float(D) ** -0.5
LN_EPS, SIM_EPS = 1e-5, 1e-6
PEN = float(2.0 ** 127)
OUT_OF_GROUP = -PEN / 2
V_GAMMA, V_BETA, V_BIAS, V_GATES = 0, S, 2 * S, 2 * S + E
VROW = 2 * S + E + 2


def build(nc, x, ctxw, vecs, route_w, w_packed, out):
    x_v = x.rearrange("(t p) d -> p t d", p=P)
    out_v = out.rearrange("(t p) d -> p t d", p=P)
    w_v = w_packed.rearrange("n p c -> p n c")
    weight_rows = nc.dram_tensor("weight_rows", (2 * E, HTOK), F32, kind="Internal").ap()

    with ExitStack() as ctx:
        def sb(name, shape, dt=F32):
            return ctx.enter_context(nc.sbuf_tensor(name, shape, dt))

        def sem(name):
            return ctx.enter_context(nc.semaphore(name))

        bank = [ctx.enter_context(nc.psum_tensor(f"bank{i}", [P, 512], F32)) for i in range(8)]
        gate_ps, up_ps = bank[0:2], bank[2:4]
        acc_ps = [bank[4:6], bank[6:8]]
        kv_ps, kvT_ps = bank[4], bank[5]
        lnT_ps = [bank[0], bank[1], bank[6], bank[7]]
        qT_ps = [bank[2], bank[3], bank[6], bank[7]]
        sim_ps = [bank[0], bank[1], bank[6], bank[7]]
        hT_ps = [bank[2], bank[3], bank[6], bank[7]]
        logitT_ps, logit_ps = [bank[4], bank[6]], [bank[5], bank[7]]
        fin_ps = [bank[4:6], bank[0:2]]

        ident = sb("ident", [P, P])
        fold = sb("fold", [2 * E, E])
        before = sb("before", [P, GROUPS, GROUPS])
        half_neg = sb("half_neg", [P, 2])
        vec = sb("vec", [P, VROW])
        gamma, beta = vec[:, V_GAMMA:V_GAMMA + S], vec[:, V_BETA:V_BETA + S]
        gates = sb("gates", [P, 2])
        cw = sb("cw", [CD + 1, B * S + CD])
        gw = sb("gw", [P, C, E])
        gw_parts = sb("gw_parts", [P, C, 2 * E], F32R)
        kv = sb("kv", [P, NT, CD])
        kvT = sb("kvT", [CD, B * S])
        xs = sb("xs", [P, NT, D])
        ln = sb("ln", [P, NT, D])
        lnT = sb("lnT", [P, B, C, S])
        qT = sb("qT", [CD, B, S])
        centred = sb("centred", [P, NT, S])
        logit = sb("logit", [P, NT, S])
        prob = sb("prob", [P, NT, S])
        x1 = sb("x1", [P, NT, D])
        hid = sb("hid", [P, NT, D])
        hT_hi = sb("hT_hi", [P, 2, C, HTOK], F32R)
        hT_lo = sb("hT_lo", [P, 2, C, HTOK], F32R)
        stats = sb("stats", [P, 3, NT, 6])
        meanvar = sb("meanvar", [P, 3, NT, 2])
        var_eps = sb("var_eps", [P, 3, NT])
        rstd = sb("rstd", [P, 3, NT])
        sim_rstd = sb("sim_rstd", [P, NT])
        neg_max = sb("neg_max", [P, NT])
        exp_sum = sb("exp_sum", [P, NT])
        exp_rec = sb("exp_rec", [P, NT])
        attn_scale = sb("attn_scale", [P, NT])
        logitT = sb("logitT", [2 * E, 2, HTOK])
        inv_score = sb("inv_score", [P, 2, HALF, E])
        score = sb("score", [P, NT, E])
        choice = sb("choice", [P, HALF, E])
        pairs = sb("pairs", [P, HALF * GROUPS, 6])
        gscore = sb("gscore", [P, HALF, GROUPS])
        beats = sb("beats", [P, HALF, GROUPS * GROUPS])
        ties = sb("ties", [P, HALF, GROUPS * GROUPS])
        rank = sb("rank", [P, HALF * GROUPS])
        masked = sb("masked", [P, HALF, E])
        top8 = sb("top8", [P, HALF, 8])
        replaced = sb("replaced", [P, HALF, E])
        picked = sb("picked", [P, HALF, E])
        pick_w = sb("pick_w", [P, HALF, E])
        w_sum = sb("w_sum", [P, HALF])
        w_rec = sb("w_rec", [P, HALF])
        w_tok = sb("w_tok", [P, 2, E, HALF])
        w_blk = sb("w_blk", [P, 2, E * HALF])
        w_raw = sb("w_raw", [P, NF, WCOL])
        w_hi, w_lo = sb("w_hi", [P, 2, WCOL], F32R), sb("w_lo", [P, 2, WCOL], F32R)
        w_row = sb("w_row", [P, 2, HTOK])
        silu_g = sb("silu_g", [P, 2, HTOK])
        weighted = sb("weighted", [P, 2, HTOK])
        act_f = sb("act_f", [P, 2, HTOK])
        act_hi, act_lo = sb("act_hi", [P, 2, HTOK], F32R), sb("act_lo", [P, 2, HTOK], F32R)
        ffnT = sb("ffnT", [P, 2, C, HTOK])

        x_in = [sem(f"x_in{b}") for b in range(B)]
        ctxw_in, vec_in, gw_in = sem("ctxw_in"), sem("vec_in"), sem("gw_in")
        w_in = [sem(f"w_in{i}") for i in range(2)]
        row_in = [sem(f"row_in{i}") for i in range(2)]
        rows_out, out_done = sem("rows_out"), sem("out_done")
        ident_ready, consts_ready = sem("ident_ready"), sem("consts_ready")
        gates_ready = sem("gates_ready")
        kv_done, kvT_done = sem("kv_done"), sem("kvT_done")
        kv_ready, kvT_ready = sem("kv_ready"), sem("kvT_ready")
        dve_order = sem("dve_order")
        var_ready, rstd_ready = sem("var_ready"), sem("rstd_ready")

        def per_batch(name):
            return [sem(f"{name}{b}") for b in range(B)]

        ln_ready, lnT_done, lnT_ready = per_batch("ln_ready"), per_batch("lnT_done"), per_batch("lnT_ready")
        qT_done, qT_ready = per_batch("qT_done"), per_batch("qT_ready")
        sim_done, sim_read = per_batch("sim_done"), per_batch("sim_read")
        max_ready, exp_ready = per_batch("max_ready"), per_batch("exp_ready")
        hid_ready, hT_done = per_batch("hid_ready"), per_batch("hT_done")
        hThi_ready, hTlo_ready = per_batch("hThi_ready"), per_batch("hTlo_ready")
        gwhi_ready, gwlo_ready = sem("gwhi_ready"), sem("gwlo_ready")
        logitT_done, logitT_ready = sem("logitT_done"), sem("logitT_ready")
        logit_done, score_ready, blk_ready = sem("logit_done"), sem("score_ready"), sem("blk_ready")
        hi_gu, hi_d = sem("hi_gu"), sem("hi_d")
        lo_gu, lo_d = sem("lo_gu"), sem("lo_d")
        gate_done, up_done, down_done = sem("gate_done"), sem("up_done"), sem("down_done")
        silu_done, weighted_done = sem("silu_done"), sem("weighted_done")
        act_done, acthi_done, actlo_done = sem("act_done"), sem("acthi_done"), sem("actlo_done")
        ffn0_ready, ffn1_ready = sem("ffn0_ready"), sem("ffn1_ready")
        fin_done, res_ready = sem("fin_done"), sem("res_ready")

        block = ctx.enter_context(nc.Block())

        def tiles(b):
            return (2 * b, 2 * b + 1)

        def each_step(eng, step, between):
            def straight(first, last):
                for k in range(first, last):
                    step(k, k % 2, k)
                    for piece in between.get(k, ()):
                        piece()

            def loop(first, last):
                with eng.Fori(first // 2, last // 2) as j:
                    for s in range(2):
                        step(2 * j + s, s, first)

            straight(0, NF + 2)
            loop(NF + 2, 2 * NF - 2)
            straight(2 * NF - 2, 2 * NF)

        @block.sync
        def _(sp):
            def load_slice(n, par):
                sp.dma_start(w_raw[:, bass.ds(n, 1), :], w_v[:, bass.ds(n, 1), :]).then_inc(w_in[par], 16)

            def load_row(row, par):
                sp.dma_start(w_row[:, par, :], weight_rows[bass.ds(row, 1), :].partition_broadcast(P)
                             .rearrange("p o t -> p (o t)")).then_inc(row_in[par], 16)

            def write_rows(h):
                sp.wait_ge(blk_ready, h + 1)
                rows = weight_rows[h * E:(h + 1) * E, :].rearrange("(c n) (t q k) -> q (n t) c k", c=2, q=4, k=32)
                for q in range(4):
                    sp.dma_start(rows[q], w_blk[32 * q:32 * q + 32, h, :].rearrange("p (c k) -> p c k", c=2))\
                      .then_inc(rows_out, 16)
                sp.wait_ge(rows_out, 64 * (h + 1))

            for b in range(B):
                sp.dma_start(xs[:, 2 * b:2 * b + 2, :], x_v[:, 2 * b:2 * b + 2, :]).then_inc(x_in[b], 16)
            ahead = 8
            for n in range(ahead):
                if n >= 2:
                    sp.wait_ge(w_in[n % 2], 16 * (n // 2))
                load_slice(n, n % 2)
            write_rows(0)
            load_row(0, 0)
            load_row(1, 1)
            with sp.Fori(ahead // 2, NF // 2) as j:
                for s in range(2):
                    sp.wait_ge(w_in[s], 16 * j)
                    load_slice(2 * j + s, s)
                    sp.wait_ge(weighted_done, 2 * j + (s + 1 - ahead))
                    load_row(2 * j + (s + 2 - ahead), s)
            with sp.Fori(NF // 2, NF // 2 + (ahead - 4) // 2) as j:
                for s in range(2):
                    sp.wait_ge(weighted_done, 2 * j + (s + 1 - ahead))
                    load_row(2 * j + (s + 2 - ahead), s)
            write_rows(1)
            with sp.Fori(E // 2, E) as j:
                for s in range(2):
                    sp.wait_ge(weighted_done, 2 * j + (s - 1))
                    load_row(2 * j + s, s)
            for b in range(B):
                sp.wait_ge(res_ready, b + 1)
                sp.dma_start(out_v[:, 2 * b:2 * b + 2, :], x1[:, 2 * b:2 * b + 2, :]).then_inc(out_done, 16)
            sp.wait_ge(out_done, 16 * B)

        @block.gpsimd
        def _(pool):
            nc.gpsimd.memset(half_neg[:], -0.5).then_inc(consts_ready, 1)
            nc.gpsimd.memset(ident[:], 0.0).then_inc(ident_ready, 1)
            pool.wait_ge(ident_ready, 1)
            nc.gpsimd.affine_select(out=ident[:], in_=ident[:], compare_op=ALU.not_equal, fill=1.0,
                                    base=0, pattern=[[-1, P]], channel_multiplier=1).then_inc(ident_ready, 1)
            nc.gpsimd.memset(before[:], 0.0).then_inc(consts_ready, 1)
            pool.wait_ge(consts_ready, 2)
            for g in range(GROUPS):
                nc.gpsimd.memset(before[:, g, g:g + 1], 0.5 - TOPK_GROUPS).then_inc(consts_ready, 1)
                if g >= 1:
                    nc.gpsimd.memset(before[:, g, 0:g], 1.0).then_inc(consts_ready, 1)
            roots = [0]

            def root(layer, b):
                roots[0] += 1
                pool.wait_ge(var_ready, roots[0])
                t = slice(2 * b, 2 * b + 2)
                nc.gpsimd.tensor_tensor(rstd[:, layer, t], var_eps[:, layer, t], half_neg[:], ALU.pow)\
                  .then_inc(rstd_ready, 1)

            def low(k, n, par, cols, high, done):
                pool.wait_ge(high, k + 1)
                nc.gpsimd.tensor_tensor(w_lo[:, par, cols], w_raw[:, bass.ds(n, 1), cols].rearrange("p o c -> p (o c)"),
                                        w_hi[:, par, cols].bitcast(F32), ALU.subtract).then_inc(done, 1)

            def low_gu(k, n, par):
                low(k, n, par, slice(0, GU), hi_gu, lo_gu)

            def low_d(k, n, par):
                low(k, n, par, slice(GU, WCOL), hi_d, lo_d)

            def step(k, par, first):
                base = 0 if first + 2 < NF else NF
                if first + 2 < 2 * NF:
                    low_gu(k + 2, k + (2 - base), par)
                base = 0 if first + 1 < NF else NF
                if first + 1 < 2 * NF:
                    low_d(k + 1, k + (1 - base), 1 - par)

            for b in range(B):
                root(0, b)
            pool.wait_ge(gwhi_ready, 1)
            nc.gpsimd.tensor_tensor(gw_parts[:, :, E:2 * E], gw[:], gw_parts[:, :, 0:E].bitcast(F32), ALU.subtract)\
              .then_inc(gwlo_ready, 1)
            low_gu(0, 0, 0)
            root(1, 0)
            root(1, 1)
            low_d(0, 0, 0)
            root(2, 0)
            root(2, 1)
            root(1, 2)
            low_gu(1, 1, 1)
            each_step(pool, step, {0: [lambda: root(1, 3)], 6: [lambda: root(2, 2)], 8: [lambda: root(2, 3)]})

        @block.scalar
        def _(act):
            act.dma_start(cw[:], ctxw).then_inc(ctxw_in, 16)
            act.dma_start(vec[:], vecs.partition_broadcast(P).rearrange("p o v -> p (o v)")).then_inc(vec_in, 16)
            act.dma_start(gw[:], route_w.rearrange("(c p) e -> p c e", p=P)).then_inc(gw_in, 16)

            def high(n, par, cols, done):
                nc.scalar.copy(w_hi[:, par, cols], w_raw[:, bass.ds(n, 1), cols].rearrange("p o c -> p (o c)"))\
                  .then_inc(done, 1)

            def high_gu(k, n, par, landed, free=True):
                if landed is not None:
                    act.wait_ge(w_in[par], landed)
                if free:
                    act.wait_ge(up_done, k - 1)
                high(n, par, slice(0, GU), hi_gu)

            def high_d(k, n, par, free=True):
                if free:
                    act.wait_ge(down_done, k - 1)
                high(n, par, slice(GU, WCOL), hi_d)

            def kvT_copy(h):
                act.wait_ge(kvT_done, h + 1)
                nc.scalar.copy(kvT[:, h * HTOK:(h + 1) * HTOK], kvT_ps[0:CD, :]).then_inc(kvT_ready, 1)

            def kv_copy(h):
                act.wait_ge(kv_done, h + 1)
                nc.scalar.copy(kv[:, HALF * h:HALF * h + HALF, :].rearrange("p t d -> p (t d)"),
                               kv_ps[:, 0:HALF * CD]).then_inc(kv_ready, 1)

            def ln_copy(b):
                act.wait_ge(lnT_done[b], 1)
                nc.scalar.copy(lnT[:, b, :, :].rearrange("p c t -> p (c t)"), lnT_ps[b][:, :])\
                  .then_inc(lnT_ready[b], 1)

            def q_copy(b):
                act.wait_ge(qT_done[b], 1)
                nc.scalar.copy(qT[:, b, :], qT_ps[b][0:CD, 0:S]).then_inc(qT_ready[b], 1)

            def softmax_exp(b):
                act.wait_ge(max_ready[b], 1)
                for t in tiles(b):
                    nc.scalar.activation(prob[:, t, :], logit[:, t, :], ACT.Exp, bias=neg_max[:, t:t + 1],
                                         accum_out=exp_sum[:, t:t + 1]).then_inc(exp_ready[b], 1)

            def hidden_high(b):
                act.wait_ge(hT_done[b], 1)
                nc.scalar.copy(hT_hi[:, b // 2, :, b % 2 * S:(b % 2 + 1) * S],
                               hT_ps[b][:, :].rearrange("p (c t) -> p c t", c=C)).then_inc(hThi_ready[b], 1)

            def logitT_copy(h):
                act.wait_ge(logitT_done, h + 1)
                nc.scalar.copy(logitT[:, h, :], logitT_ps[h][0:2 * E, :]).then_inc(logitT_ready, 1)

            def logit_exp(h):
                act.wait_ge(logit_done, h + 1)
                nc.scalar.activation(inv_score[:, h, :, :], logit_ps[h][:, 0:HALF * E].rearrange("p (t e) -> p t e", e=E),
                                     ACT.Exp, scale=-1.0).then_inc(score_ready, 1)

            def step(k, par, first):
                act.wait_ge(gate_done, k + 1)
                if first >= 2:
                    act.wait_ge(act_done, k - 1)
                nc.scalar.activation(silu_g[:, par, :], gate_ps[par][:, :], ACT.Silu).then_inc(silu_done, 1)
                base = 0 if first + 2 < NF else NF
                if first + 2 < 2 * NF:
                    high_gu(k + 2, k + (2 - base), par, None if base else 8 * (k + (2 - par)) + 16)
                act.wait_ge(act_done, k + 1)
                if first >= 2:
                    act.wait_ge(down_done, k - 1)
                nc.scalar.copy(act_hi[:, par, :], act_f[:, par, :]).then_inc(acthi_done, 1)
                base = 0 if first + 1 < NF else NF
                if first + 1 < 2 * NF:
                    high_d(k + 1, k + (1 - base), 1 - par, first >= 1)

            def ffn_copy(h):
                act.wait_ge(down_done, NF * (h + 1))
                nc.scalar.copy(ffnT[:, h, 0, :], acc_ps[h][0][:, :]).then_inc(ffn0_ready, 1)

            act.wait_ge(vec_in, 16)
            nc.scalar.activation(gates[:], vec[:, V_GATES:V_GATES + 2], ACT.Tanh).then_inc(gates_ready, 1)
            act.wait_ge(gw_in, 16)
            nc.scalar.copy(gw_parts[:, :, 0:E], gw[:]).then_inc(gwhi_ready, 1)
            kv_copy(0)
            kvT_copy(0)
            ln_copy(0)
            ln_copy(1)
            q_copy(0)
            q_copy(1)
            kv_copy(1)
            kvT_copy(1)
            high_gu(0, 0, 0, 16, False)
            ln_copy(2)
            ln_copy(3)
            q_copy(2)
            q_copy(3)
            high_d(0, 0, 0, False)
            high_gu(1, 1, 1, 16, False)
            softmax_exp(0)
            softmax_exp(1)
            hidden_high(0)
            hidden_high(1)
            logitT_copy(0)
            logit_exp(0)
            each_step(act, step, {
                4: [lambda: softmax_exp(2), lambda: softmax_exp(3)],
                10: [lambda: hidden_high(2)],
                11: [lambda: hidden_high(3)],
                12: [lambda: logitT_copy(1)],
                13: [lambda: logit_exp(1)],
                NF: [lambda: ffn_copy(0)],
            })
            ffn_copy(1)

        @block.vector
        def _(dve):
            order = [0]

            def link(ins):
                order[0] += 1
                ins.then_inc(dve_order, 1)
                dve.wait_ge(dve_order, order[0])

            def mean_var(layer, b, source, scale2, eps):
                for t in tiles(b):
                    ins = nc.vector.bn_stats(stats[:, layer, t, :], source(t))
                link(ins)
                for t in tiles(b):
                    ins = nc.vector.bn_aggr(meanvar[:, layer, t, :], stats[:, layer, t, :])
                link(ins)
                ts = slice(2 * b, 2 * b + 2)
                nc.vector.tensor_scalar(var_eps[:, layer, ts], meanvar[:, layer, ts, 1], scale2, eps,
                                        ALU.mult, ALU.add).then_inc(var_ready, 1)

            def normalise(layer, b, n_root, source, dst, ready):
                dve.wait_ge(rstd_ready, n_root)
                for t in tiles(b):
                    nc.vector.tensor_scalar(dst[:, t, :], source[:, t, :], meanvar[:, layer, t, 0:1],
                                            rstd[:, layer, t:t + 1], ALU.subtract, ALU.mult).then_inc(ready[b], 1)

            def x_stats(b):
                dve.wait_ge(x_in[b], 16)
                mean_var(0, b, lambda t: xs[:, t, :], 1.0, LN_EPS)

            def sim_of(b, t):
                return sim_ps[b][:, (t % 2) * S:(t % 2 + 1) * S]

            def sim_stats(b):
                dve.wait_ge(sim_done[b], 1)
                mean_var(1, b, lambda t: sim_of(b, t), SIM_SCALE ** 2, SIM_EPS)

            def sim_centre(b):
                for t in tiles(b):
                    nc.vector.scalar_tensor_tensor(centred[:, t, :], sim_of(b, t), meanvar[:, 1, t, 0:1], gamma,
                                                   ALU.subtract, ALU.mult).then_inc(sim_read[b], 1)

            def sim_logits(b, n_root):
                ts = slice(2 * b, 2 * b + 2)
                dve.wait_ge(rstd_ready, n_root)
                link(nc.vector.tensor_scalar(sim_rstd[:, ts], rstd[:, 1, ts], SIM_SCALE, None, ALU.mult))
                dve.wait_ge(sim_read[b], 2)
                for t in tiles(b):
                    ins = nc.vector.scalar_tensor_tensor(logit[:, t, :], centred[:, t, :], sim_rstd[:, t:t + 1],
                                                         beta, ALU.mult, ALU.add)
                link(ins)
                nc.vector.tensor_reduce(neg_max[:, ts], logit[:, ts, :], AX.X, ALU.max, negate=True)\
                  .then_inc(max_ready[b], 1)

            def residual(b):
                ts = slice(2 * b, 2 * b + 2)
                dve.wait_ge(exp_ready[b], 2)
                link(nc.vector.reciprocal(exp_rec[:, ts], exp_sum[:, ts]))
                link(nc.vector.tensor_scalar(attn_scale[:, ts], exp_rec[:, ts], gates[:, 0:1], None, ALU.mult))
                for t in tiles(b):
                    ins = nc.vector.scalar_tensor_tensor(x1[:, t, :], prob[:, t, :], attn_scale[:, t:t + 1],
                                                         xs[:, t, :], ALU.mult, ALU.add)
                link(ins)

            def x1_stats(b):
                mean_var(2, b, lambda t: x1[:, t, :], 1.0, LN_EPS)

            def hidden_low(b):
                dve.wait_ge(hThi_ready[b], 1)
                cols = slice(b % 2 * S, (b % 2 + 1) * S)
                nc.vector.tensor_tensor(hT_lo[:, b // 2, :, cols], hT_ps[b][:, :].rearrange("p (c t) -> p c t", c=C),
                                        hT_hi[:, b // 2, :, cols].bitcast(F32), ALU.subtract)\
                  .then_inc(hTlo_ready[b], 1)

            def step(k, par, first):
                dve.wait_ge(silu_done, k + 1)
                gated = silu_g
                if not (first < NSH or NF <= first < NF + NSH):
                    routed = k + (1 - NSH if first < NF else 1 - 2 * NSH)
                    dve.wait_ge(row_in[par], 8 * (routed + (1 - par)))
                    nc.vector.tensor_tensor(weighted[:, par, :], silu_g[:, par, :], w_row[:, par, :], ALU.mult)\
                      .then_inc(weighted_done, 1)
                    dve.wait_ge(weighted_done, routed)
                    gated = weighted
                dve.wait_ge(up_done, k + 1)
                if first >= 2:
                    dve.wait_ge(actlo_done, k - 1)
                nc.vector.tensor_tensor(act_f[:, par, :], up_ps[par][:, :], gated[:, par, :], ALU.mult)\
                  .then_inc(act_done, 1)
                dve.wait_ge(acthi_done, k + 1)
                if first >= 2:
                    dve.wait_ge(down_done, k - 1)
                nc.vector.tensor_tensor(act_lo[:, par, :], act_f[:, par, :], act_hi[:, par, :].bitcast(F32),
                                        ALU.subtract).then_inc(actlo_done, 1)

            member = choice[:].rearrange("p t (g m) -> p (t g) m", g=GROUPS)

            def rank_groups(h):
                def grid(a):
                    return a.rearrange("p t (g h) -> p t g h", g=GROUPS)

                dve.wait_ge(score_ready, h + 1)
                bias = vec[:, V_BIAS:V_BIAS + E].unsqueeze(1).to_broadcast([P, HALF, E])
                link(nc.vector.tensor_scalar(inv_score[:, h], inv_score[:, h], 1.0, None, ALU.add))
                link(nc.vector.reciprocal(score[:, HALF * h:HALF * h + HALF, :], inv_score[:, h]))
                link(nc.vector.tensor_tensor(choice[:], score[:, HALF * h:HALF * h + HALF, :], bias, ALU.add))
                nc.vector.tensor_tensor(pairs[:, :, 0:3], member[:, :, 0:3], member[:, :, 1:4], ALU.add)
                nc.vector.tensor_tensor(pairs[:, :, 3:5], member[:, :, 0:2], member[:, :, 2:4], ALU.add)
                link(nc.vector.tensor_tensor(pairs[:, :, 5:6], member[:, :, 0:1], member[:, :, 3:4], ALU.add))
                link(nc.vector.tensor_reduce(gscore[:].rearrange("p t g -> p (t g)"), pairs[:], AX.X, ALU.max))
                other = gscore[:].unsqueeze(2).to_broadcast([P, HALF, GROUPS, GROUPS])
                own = gscore[:].unsqueeze(3).to_broadcast([P, HALF, GROUPS, GROUPS])
                nc.vector.tensor_tensor(grid(beats[:]), other, own, ALU.is_gt)
                link(nc.vector.tensor_tensor(grid(ties[:]), other, own, ALU.is_equal))
                earlier = before[:].rearrange("p g h -> p (g h)").unsqueeze(1).to_broadcast([P, HALF, GROUPS * GROUPS])
                link(nc.vector.tensor_tensor(ties[:], ties[:], earlier, ALU.mult))
                link(nc.vector.tensor_tensor(beats[:], beats[:], ties[:], ALU.add))
                link(nc.vector.tensor_reduce(rank[:], beats[:].rearrange("p t (g h) -> p (t g) h", g=GROUPS),
                                             AX.X, ALU.add))

            def mask_groups():
                link(nc.vector.scalar_tensor_tensor(masked[:].rearrange("p t (g m) -> p (t g) m", g=GROUPS),
                                                    rank[:].unsqueeze(2).to_broadcast([P, HALF * GROUPS, E // GROUPS]),
                                                    -PEN, member, ALU.mult, ALU.min))
                for t in range(HALF):
                    ins = nc.vector.max(top8[:, t, :], masked[:, t, :])
                link(ins)
                link(nc.vector.memset(top8[:, :, TOPK:8], OUT_OF_GROUP))
                for t in range(HALF):
                    ins = nc.vector.match_replace(replaced[:, t, :], top8[:, t, :], masked[:, t, :], OUT_OF_GROUP)
                link(ins)

            def pick_experts(h):
                link(nc.vector.tensor_tensor(picked[:], masked[:], replaced[:], ALU.not_equal))
                link(nc.vector.tensor_tensor(pick_w[:], picked[:], score[:, HALF * h:HALF * h + HALF, :], ALU.mult))
                link(nc.vector.tensor_reduce(w_sum[:], pick_w[:], AX.X, ALU.add))
                link(nc.vector.tensor_scalar(w_sum[:], w_sum[:], 1.0 / ROUTED_SCALE, 1e-20 / ROUTED_SCALE,
                                             ALU.mult, ALU.add))
                link(nc.vector.reciprocal(w_rec[:], w_sum[:]))
                link(nc.vector.tensor_tensor(w_tok[:, h, :, :].rearrange("p e t -> p t e"), pick_w[:],
                                             w_rec[:].unsqueeze(2).to_broadcast([P, HALF, E]), ALU.mult))
                nc.vector.transpose(w_blk[:, h, :], w_tok[:, h, :, :].rearrange("p e t -> p (e t)"))\
                  .then_inc(blk_ready, 1)

            def ffn_copy(h):
                dve.wait_ge(down_done, NF * (h + 1))
                nc.vector.tensor_copy(ffnT[:, h, 1, :], acc_ps[h][1][:, :]).then_inc(ffn1_ready, 1)

            def result(h):
                for b in range(2):
                    t = HALF * h + 2 * b
                    dve.wait_ge(fin_done, 2 * h + b + 1)
                    nc.vector.scalar_tensor_tensor(x1[:, t:t + 2, :].rearrange("p t d -> p (t d)"),
                                                   fin_ps[h][b][:, :], gates[:, 1:2],
                                                   x1[:, t:t + 2, :].rearrange("p t d -> p (t d)"),
                                                   ALU.mult, ALU.add).then_inc(res_ready, 1)

            x_stats(0)
            x_stats(1)
            normalise(0, 0, 1, xs, ln, ln_ready)
            normalise(0, 1, 2, xs, ln, ln_ready)
            dve.wait_ge(ident_ready, 2)
            nc.vector.tensor_tensor(fold[:], ident[0:2 * E, 0:E], ident[0:2 * E, E:2 * E], ALU.add)\
              .then_inc(ident_ready, 1)
            x_stats(2)
            x_stats(3)
            normalise(0, 2, 3, xs, ln, ln_ready)
            normalise(0, 3, 4, xs, ln, ln_ready)
            dve.wait_ge(vec_in, 16)
            sim_stats(0)
            sim_centre(0)
            sim_stats(1)
            sim_centre(1)
            sim_logits(0, 5)
            sim_logits(1, 6)
            dve.wait_ge(gates_ready, 1)
            residual(0)
            x1_stats(0)
            residual(1)
            x1_stats(1)
            normalise(2, 0, 7, x1, hid, hid_ready)
            normalise(2, 1, 8, x1, hid, hid_ready)
            hidden_low(0)
            hidden_low(1)
            sim_stats(2)
            sim_centre(2)
            dve.wait_ge(consts_ready, 2 + 2 * GROUPS - 1)
            rank_groups(0)
            mask_groups()
            pick_experts(0)
            each_step(dve, step, {
                0: [lambda: sim_stats(3)],
                1: [lambda: sim_centre(3)],
                2: [lambda: sim_logits(2, 9)],
                3: [lambda: sim_logits(3, 10)],
                5: [lambda: residual(2)],
                6: [lambda: x1_stats(2)],
                7: [lambda: residual(3)],
                8: [lambda: x1_stats(3)],
                9: [lambda: normalise(2, 2, 11, x1, hid, hid_ready)],
                10: [lambda: normalise(2, 3, 12, x1, hid, hid_ready), lambda: hidden_low(2)],
                11: [lambda: hidden_low(3)],
                14: [lambda: rank_groups(1)],
                15: [mask_groups],
                16: [lambda: pick_experts(1)],
                NF: [lambda: ffn_copy(0)],
                NF + 1: [lambda: result(0)],
            })
            ffn_copy(1)
            result(1)

        @block.tensor
        def _(pe):
            wk = cw[:, B * S:B * S + CD]

            def project(h):
                for t in range(HALF):
                    last = nc.tensor.matmul(kv_ps[:, t * CD:(t + 1) * CD], cw[:, (HALF * h + t) * P:(HALF * h + t + 1) * P],
                                            wk, start=True, stop=True)
                last.then_inc(kv_done, 1)
                nc.tensor.matmul(kvT_ps[0:CD, :], wk, cw[:, h * HTOK:(h + 1) * HTOK], start=True, stop=True)\
                  .then_inc(kvT_done, 1)

            def transposes(b, dst, source, ready, done):
                for i, t in enumerate(tiles(b)):
                    pe.wait_ge(ready[b], i + 1)
                    for c in range(C):
                        last = nc.tensor.transpose(dst[b][:, c * S + i * P:c * S + (i + 1) * P],
                                                   source[:, t, c * P:(c + 1) * P], ident[:])
                last.then_inc(done[b], 1)

            def query(b):
                pe.wait_ge(lnT_ready[b], 1)
                pe.wait_ge(kv_ready, b // 2 + 1)
                for c in range(C):
                    last = nc.tensor.matmul(qT_ps[b][0:CD, 0:S], kv[:, 2 * b + c, :], lnT[:, b, c, :],
                                            start=(c == 0), stop=(c == C - 1))
                last.then_inc(qT_done[b], 1)

            def similarity(b):
                pe.wait_ge(qT_ready[b], 1)
                pe.wait_ge(kvT_ready, b // 2 + 1)
                for i in range(2):
                    last = nc.tensor.matmul(sim_ps[b][:, i * S:(i + 1) * S], qT[:, b, i * P:(i + 1) * P],
                                            kvT[:, b * S:(b + 1) * S], start=True, stop=True)
                last.then_inc(sim_done[b], 1)

            def hidden(b):
                pe.wait_ge(sim_read[b], 2)
                transposes(b, hT_ps, hid, hid_ready, hT_done)

            def route(h):
                for b in (2 * h, 2 * h + 1):
                    pe.wait_ge(hTlo_ready[b], 1)
                pe.wait_ge(gwlo_ready, 1)
                pe.wait_ge(kv_ready, 2)
                pe.wait_ge(kvT_ready, 2)
                moving = [(c, m) for c in range(C) for m in (hT_hi, hT_lo)]
                for i, (c, m) in enumerate(moving):
                    last = nc.tensor.matmul(logitT_ps[h][0:2 * E, :], gw_parts[:, c, :], m[:, h, c, :],
                                            start=(i == 0), stop=(i == len(moving) - 1))
                last.then_inc(logitT_done, 1)

            def route_back(h):
                pe.wait_ge(logitT_ready, h + 1)
                pe.wait_ge(ident_ready, 3)
                for t in range(HALF):
                    last = nc.tensor.matmul(logit_ps[h][:, t * E:(t + 1) * E], logitT[:, h, t * P:(t + 1) * P],
                                            fold[:], start=True, stop=True)
                last.then_inc(logit_done, 1)

            def product(dst, w0, moving, par):
                for i, (m_hi, m_lo) in enumerate(moving):
                    cols = slice(w0 + i * P, w0 + (i + 1) * P)
                    for r, (w, m) in enumerate(((w_hi, m_hi), (w_hi, m_lo), (w_lo, m_hi))):
                        last = nc.tensor.matmul(dst, w[:, par, cols], m, start=i == r == 0,
                                                stop=i == len(moving) - 1 and r == 2, skip_group_check=True)
                return last

            def gate_up(k, par, half, first):
                pe.wait_ge(hi_gu, k + 1)
                pe.wait_ge(lo_gu, k + 1)
                moving = [(hT_hi[:, half, c, :], hT_lo[:, half, c, :]) for c in range(C)]
                if first >= 2:
                    pe.wait_ge(silu_done, k - 1)
                product(gate_ps[par][:, :], 0, moving, par).then_inc(gate_done, 1)
                if first >= 2:
                    pe.wait_ge(act_done, k - 1)
                product(up_ps[par][:, :], C * P, moving, par).then_inc(up_done, 1)

            def down(k, par, half, start):
                pe.wait_ge(hi_d, k + 1)
                pe.wait_ge(acthi_done, k + 1)
                parts = ((w_hi, act_hi, None), (w_lo, act_hi, lo_d), (w_hi, act_lo, actlo_done))
                for i, (w, m, ready) in enumerate(parts):
                    if ready is not None:
                        pe.wait_ge(ready, k + 1)
                    for c in range(C):
                        cols = slice(GU + c * P, GU + (c + 1) * P)
                        last = nc.tensor.matmul(acc_ps[half][c][:, :], w[:, par, cols], m[:, par, :],
                                                start=start and i == 0, stop=i == 2, skip_group_check=True)
                last.then_inc(down_done, 1)

            def step(k, par, first):
                gate_up(k, par, int(first >= NF), first)
                if first == 1:
                    pe.wait_ge(score_ready, 1)
                if first == NF + 1:
                    pe.wait_ge(score_ready, 2)
                if first >= 1:
                    down(k - 1, 1 - par, int(first - 1 >= NF), first - 1 in (0, NF))

            def finish(h):
                pe.wait_ge(ffn0_ready, h + 1)
                pe.wait_ge(ffn1_ready, h + 1)
                for b in range(2):
                    if h == 1:
                        pe.wait_ge(silu_done, 2 * NF - 1 + b)
                    for i in range(2):
                        for c in range(C):
                            tok = slice((2 * b + i) * P, (2 * b + i + 1) * P)
                            last = nc.tensor.transpose(fin_ps[h][b][:, i * D + c * P:i * D + (c + 1) * P],
                                                       ffnT[:, h, c, tok], ident[:])
                    last.then_inc(fin_done, 1)

            pe.wait_ge(ctxw_in, 16)
            project(0)
            pe.wait_ge(ident_ready, 2)
            transposes(0, lnT_ps, ln, ln_ready, lnT_done)
            transposes(1, lnT_ps, ln, ln_ready, lnT_done)
            query(0)
            query(1)
            similarity(0)
            similarity(1)
            pe.wait_ge(kvT_ready, 1)
            project(1)
            transposes(2, lnT_ps, ln, ln_ready, lnT_done)
            transposes(3, lnT_ps, ln, ln_ready, lnT_done)
            for b in (2, 3):
                query(b)
            for b in (2, 3):
                similarity(b)
            hidden(0)
            hidden(1)
            route(0)
            route_back(0)
            each_step(pe, step, {
                10: [lambda: hidden(2)],
                11: [lambda: hidden(3)],
                12: [lambda: route(1)],
                13: [lambda: route_back(1)],
                NF + 1: [lambda: finish(0)],
            })
            down(2 * NF - 1, 1, 1, False)
            finish(1)


def kernel(x, ctx_512, g_xattn, g_ffn, L0_xattn_W_k, L0_xattn_b_k, L0_xattn_ln_gamma, L0_xattn_ln_beta,
           L0_ffn_gate_weight, L0_ffn_e_score_correction_bias, L0_ffn_gate_w, L0_ffn_up_w, L0_ffn_down_w,
           L0_ffn_sh_gate_w, L0_ffn_sh_up_w, L0_ffn_sh_down_w):
    import numpy as np
    import concourse.bacc as bacc
    from concourse.bass_utils import run_bass_kernel_spmd as run

    def arr(a):
        return np.asarray(a)

    def slices(gate, up, down):
        n = gate.shape[0]
        parts = [w.transpose(0, 2, 1).reshape(n, C, P, P).transpose(0, 2, 1, 3).reshape(n, P, C * P)
                 for w in (gate, up)]
        return np.concatenate(parts + [down.transpose(0, 2, 1)], axis=2)

    tokens = B * S
    ctxT = arr(ctx_512).reshape(tokens, CD).T
    ones = np.ones((1, tokens), np.float32)
    wk = np.concatenate([arr(L0_xattn_W_k).T, arr(L0_xattn_b_k).reshape(1, CD)], axis=0)
    sh = slices(arr(L0_ffn_sh_gate_w).reshape(NSH, P, D), arr(L0_ffn_sh_up_w).reshape(NSH, P, D),
                arr(L0_ffn_sh_down_w).reshape(D, NSH, P).transpose(1, 0, 2))
    arrays = {
        "x_in": arr(x).reshape(tokens, D),
        "ctxw_in": np.concatenate([np.concatenate([ctxT, ones], axis=0), wk], axis=1),
        "vecs_in": np.concatenate([arr(a).reshape(-1) for a in (
            L0_xattn_ln_gamma, L0_xattn_ln_beta, L0_ffn_e_score_correction_bias, g_xattn, g_ffn)]).reshape(1, -1),
        "route_in": arr(L0_ffn_gate_weight).T,
        "w_in": np.concatenate([sh, slices(arr(L0_ffn_gate_w), arr(L0_ffn_up_w), arr(L0_ffn_down_w))], axis=0),
    }
    arrays = {k: np.ascontiguousarray(v) for k, v in arrays.items()}
    nc = bacc.Bacc("TRN2", target_bir_lowering=False, num_devices=1)
    args = [nc.dram_tensor(k, v.shape, F32, kind="ExternalInput").ap() for k, v in arrays.items()]
    out = nc.dram_tensor("out", (tokens, D), F32, kind="ExternalOutput").ap()
    build(nc, *args, out)
    r = run(nc, [arrays], core_ids=[0])
    return r.results[0]["out"].reshape(B, S, D)
```

```python
from contextlib import ExitStack

import concourse.bass as bass
from concourse import mybir

F32 = mybir.dt.float32
F32R = mybir.dt.float32r
ALU = mybir.AluOpType
ACT = mybir.ActivationFunctionType
AX = mybir.AxisListType

P = 128
B, S, D = 4, 256, 256
CD = 64
E, FE = 16, 128
FS = 256
GROUPS, TOPK_GROUPS, TOPK = 4, 2, 4
ROUTED_SCALE = 2.5
NT = B * S // P
HALF = 4
HTOK = HALF * P
C = D // P
NSH = FS // P
NF = NSH + E
WCOL = 2 * C * P + D
GU = 2 * C * P
SIM_SCALE = float(D) ** -0.5
LN_EPS, SIM_EPS = 1e-5, 1e-6
PEN = float(2.0 ** 127)
OUT_OF_GROUP = -PEN / 2
WEIGHTED_LAST = (NSH, NSH + 1)
V_GAMMA, V_BETA, V_BIAS, V_GATES = 0, S, 2 * S, 2 * S + E
VROW = 2 * S + E + 2


def build(nc, x, ctxw, vecs, route_w, w_packed, out):
    x_v = x.rearrange("(t p) d -> p t d", p=P)
    out_v = out.rearrange("(t p) d -> p t d", p=P)
    w_v = w_packed.rearrange("n p c -> p n c")
    weight_rows = nc.dram_tensor("weight_rows", (2 * E, HTOK), F32, kind="Internal").ap()

    with ExitStack() as ctx:
        def sb(name, shape, dt=F32):
            return ctx.enter_context(nc.sbuf_tensor(name, shape, dt))

        def sem(name):
            return ctx.enter_context(nc.semaphore(name))

        bank = [ctx.enter_context(nc.psum_tensor(f"bank{i}", [P, 512], F32)) for i in range(8)]
        gate_ps, up_ps = bank[0:2], bank[2:4]
        acc_ps = [bank[4:6], bank[6:8]]
        kv_ps, kvT_ps = bank[4], bank[5]
        lnT_ps = [bank[0], bank[1], bank[6], bank[7]]
        qT_ps = [bank[2], bank[3], bank[6], bank[7]]
        sim_ps = [bank[0], bank[1], bank[6], bank[7]]
        hT_ps = [bank[2], bank[3], bank[6], bank[7]]
        logitT_ps, logit_ps = [bank[4], bank[6]], [bank[5], bank[7]]
        first_row_ps = bank[6]
        fin_ps = [bank[4], bank[5], bank[0], bank[1]]

        ident = sb("ident", [P, P])
        before = sb("before", [P, GROUPS, GROUPS])
        zeros = sb("zeros", [P, HTOK], F32R)
        half_neg = sb("half_neg", [P, 2])
        vec = sb("vec", [P, VROW])
        gamma, beta = vec[:, V_GAMMA:V_GAMMA + S], vec[:, V_BETA:V_BETA + S]
        gamma_scaled = sb("gamma_scaled", [P, S])
        gates = sb("gates", [P, 2])
        cw = sb("cw", [CD + 1, B * S + CD])
        gw = sb("gw", [P, C, E])
        gw_parts = sb("gw_parts", [P, C, 2 * E], F32R)
        kv = sb("kv", [P, NT, CD])
        kvT = sb("kvT", [CD, B * S])
        xs = sb("xs", [P, NT, D])
        ln = sb("ln", [P, NT, D])
        lnT = sb("lnT", [P, B, C, S])
        qT = sb("qT", [CD, B, S])
        centred = sb("centred", [P, NT, S])
        logit = sb("logit", [P, NT, S])
        prob = sb("prob", [P, NT, S])
        x1 = sb("x1", [P, NT, D])
        hid = ln
        hT_hi = sb("hT_hi", [P, 2, C, HTOK], F32R)
        hT_lo = sb("hT_lo", [P, 2, C, HTOK], F32R)
        stats = sb("stats", [P, 3, NT, 6])
        meanvar = sb("meanvar", [P, 3, NT, 2])
        var_eps = sb("var_eps", [P, 3, NT])
        rstd = sb("rstd", [P, 3, NT])
        shift = sb("shift", [P, HALF])
        neg_max = sb("neg_max", [P, NT])
        exp_sum = sb("exp_sum", [P, NT])
        exp_rec = sb("exp_rec", [P, NT])
        attn_scale = sb("attn_scale", [P, NT])
        logitT = sb("logitT", [2 * E, 2, HTOK])
        route_logit = sb("route_logit", [P, 2, HALF, E])
        inv_score = sb("inv_score", [P, 2, HALF, E])
        score = sb("score", [P, NT, E])
        choice = sb("choice", [P, HALF, E])
        pairs = sb("pairs", [P, HALF * GROUPS, 6])
        gscore = sb("gscore", [P, HALF, GROUPS])
        beats = sb("beats", [P, HALF, GROUPS * GROUPS])
        ties = sb("ties", [P, HALF, GROUPS * GROUPS])
        rank = sb("rank", [P, HALF * GROUPS])
        masked = sb("masked", [P, HALF, E])
        top8 = sb("top8", [P, HALF, 8])
        replaced = sb("replaced", [P, HALF, E])
        picked = sb("picked", [P, HALF, E])
        pick_w = sb("pick_w", [P, HALF, E])
        w_sum = sb("w_sum", [P, HALF])
        w_rec = sb("w_rec", [P, HALF])
        w_tok = sb("w_tok", [P, 2, E, HALF])
        w_blk = sb("w_blk", [P, 2, E * HALF])
        w_raw = sb("w_raw", [P, NF, WCOL])
        w_hi, w_lo = sb("w_hi", [P, 2, WCOL], F32R), sb("w_lo", [P, 2, WCOL], F32R)
        w_row = sb("w_row", [P, 2, HTOK])
        silu_g = sb("silu_g", [P, 2, HTOK])
        weighted = sb("weighted", [P, 2, HTOK])
        act_f = sb("act_f", [P, 2, HTOK])
        act_hi, act_lo = sb("act_hi", [P, 2, HTOK], F32R), sb("act_lo", [P, 2, HTOK], F32R)
        ffnT = sb("ffnT", [P, 2, C, HTOK])

        x_in = [sem(f"x_in{b}") for b in range(B)]
        ctxw_in, vec_in, gw_in = sem("ctxw_in"), sem("vec_in"), sem("gw_in")
        w_in = [sem(f"w_in{i}") for i in range(2)]
        row_in = [sem(f"row_in{i}") for i in range(2)]
        rows_out = [sem(f"rows_out{c}") for c in range(2)]
        out_done = sem("out_done")
        ident_ready, consts_ready = sem("ident_ready"), sem("consts_ready")
        gates_ready, zeros_ready, warm_done = sem("gates_ready"), sem("zeros_ready"), sem("warm_done")
        kv_done, kvT_done = sem("kv_done"), sem("kvT_done")
        kv_ready, kvT_ready = sem("kv_ready"), sem("kvT_ready")
        dve_order = sem("dve_order")
        var_ready, rstd_ready = sem("var_ready"), sem("rstd_ready")

        def per_batch(name):
            return [sem(f"{name}{b}") for b in range(B)]

        ln_ready, lnT_done, lnT_ready = per_batch("ln_ready"), per_batch("lnT_done"), per_batch("lnT_ready")
        qT_done, qT_ready = per_batch("qT_done"), per_batch("qT_ready")
        sim_done, sim_read = per_batch("sim_done"), per_batch("sim_read")
        logits_ready, scale_ready, x1_ready = per_batch("logits_ready"), per_batch("scale_ready"), per_batch("x1_ready")
        max_ready, exp_ready = per_batch("max_ready"), per_batch("exp_ready")
        hid_ready, hT_done = per_batch("hid_ready"), per_batch("hT_done")
        hThi_ready, hTlo_ready = per_batch("hThi_ready"), per_batch("hTlo_ready")
        scaled_ready, gamma_ready, shift_ready = sem("scaled_ready"), sem("gamma_ready"), sem("shift_ready")
        gwhi_ready, gwlo_ready = sem("gwhi_ready"), sem("gwlo_ready")
        logitT_done, logitT_ready = sem("logitT_done"), sem("logitT_ready")
        logit_done, route_logit_ready, score_ready = sem("logit_done"), sem("route_logit_ready"), sem("score_ready")
        weights_ready, blk_ready, first_row_done = sem("weights_ready"), sem("blk_ready"), sem("first_row_done")
        hi_gu, hi_d = sem("hi_gu"), sem("hi_d")
        lo_gu, lo_d = sem("lo_gu"), sem("lo_d")
        gate_done, up_done, down_done = sem("gate_done"), sem("up_done"), sem("down_done")
        silu_done, weighted_done = sem("silu_done"), sem("weighted_done")
        act_done, acthi_done, actlo_done = sem("act_done"), sem("acthi_done"), sem("actlo_done")
        ffn0_ready, ffn1_ready = sem("ffn0_ready"), sem("ffn1_ready")
        fin_done, res_ready = sem("fin_done"), sem("res_ready")

        block = ctx.enter_context(nc.Block())

        def tiles(b):
            return (2 * b, 2 * b + 1)

        def batch_cols(b):
            return slice(b % 2 * S, (b % 2 + 1) * S)

        def spans(first):
            return (slice(0, S), slice(S, HTOK)) if first == 2 * NF - 1 else (slice(0, HTOK),)

        def summed(b):
            return NF if b < 2 else 2 * NF + 1

        def each_step(eng, step, between):
            def straight(first, last):
                for k in range(first, last):
                    step(k, k % 2, k)
                    for piece in between.get(k, ()):
                        piece()

            def loop(first, last):
                with eng.Fori(first // 2, last // 2) as j:
                    for s in range(2):
                        step(2 * j + s, s, first)

            straight(0, NF + 2)
            loop(NF + 2, 2 * NF - 2)
            straight(2 * NF - 2, 2 * NF)

        @block.sync
        def _(sp):
            def load_slice(n, par):
                sp.dma_start(w_raw[:, bass.ds(n, 1), :], w_v[:, bass.ds(n, 1), :]).then_inc(w_in[par], 16)

            def load_row(row, par):
                sp.dma_start(w_row[:, par, :], weight_rows[bass.ds(row, 1), :].partition_broadcast(P)
                             .rearrange("p o t -> p (o t)")).then_inc(row_in[par], 16)

            def write_rows(h):
                sp.wait_ge(blk_ready, h + 1)
                rows = weight_rows[h * E:(h + 1) * E, :].rearrange("(c n) (t q k) -> c q (n t) k", c=2, q=4, k=32)
                for c in range(2):
                    sp.dma_start(rows[c], w_blk[:, h, 32 * c:32 * c + 32]).then_inc(rows_out[c], 16)

            for b in range(B):
                sp.dma_start(xs[:, 2 * b:2 * b + 2, :], x_v[:, 2 * b:2 * b + 2, :]).then_inc(x_in[b], 16)
            ahead = 8
            for n in range(ahead):
                if n >= 2:
                    sp.wait_ge(w_in[n % 2], 16 * (n // 2))
                load_slice(n, n % 2)
            write_rows(0)
            sp.wait_ge(rows_out[0], 16)
            load_row(1, 1)
            sp.wait_ge(rows_out[1], 16)
            with sp.Fori(ahead // 2, NF // 2) as j:
                for s in range(2):
                    sp.wait_ge(w_in[s], 16 * j)
                    load_slice(2 * j + s, s)
                    sp.wait_ge(act_done, 2 * j + (s + 1 - ahead + NSH))
                    load_row(2 * j + (s + 2 - ahead), s)
            with sp.Fori(NF // 2, NF // 2 + (E - 2 - (NF - ahead)) // 2) as j:
                for s in range(2):
                    sp.wait_ge(act_done, 2 * j + (s + 1 - ahead + NSH))
                    load_row(2 * j + (s + 2 - ahead), s)
            write_rows(1)
            for c in range(2):
                sp.wait_ge(rows_out[c], 32)
            with sp.Fori(E // 2, E) as j:
                for s in range(2):
                    sp.wait_ge(act_done, 2 * j + (s - 1 + 2 * NSH))
                    load_row(2 * j + s, s)
            for b in range(B):
                sp.wait_ge(res_ready, b + 1)
                sp.dma_start(out_v[:, 2 * b:2 * b + 2, :], x1[:, 2 * b:2 * b + 2, :]).then_inc(out_done, 16)
            sp.wait_ge(out_done, 16 * B)

        @block.gpsimd
        def _(pool):
            nc.gpsimd.memset(half_neg[:], -0.5).then_inc(consts_ready, 1)
            nc.gpsimd.memset(ident[:], 0.0).then_inc(ident_ready, 1)
            pool.wait_ge(ident_ready, 1)
            nc.gpsimd.affine_select(out=ident[:], in_=ident[:], compare_op=ALU.not_equal, fill=1.0,
                                    base=0, pattern=[[-1, P]], channel_multiplier=1).then_inc(ident_ready, 1)
            nc.gpsimd.memset(before[:], 0.0).then_inc(consts_ready, 1)
            pool.wait_ge(consts_ready, 2)
            for g in range(GROUPS):
                nc.gpsimd.memset(before[:, g, g:g + 1], 0.5 - TOPK_GROUPS).then_inc(consts_ready, 1)
                if g >= 1:
                    nc.gpsimd.memset(before[:, g, 0:g], 1.0).then_inc(consts_ready, 1)
            roots = [0]

            def root(layer, b):
                roots[0] += 1
                pool.wait_ge(var_ready, roots[0])
                t = slice(2 * b, 2 * b + 2)
                nc.gpsimd.tensor_tensor(rstd[:, layer, t], var_eps[:, layer, t], half_neg[:], ALU.pow)\
                  .then_inc(rstd_ready, 1)

            def low(k, n, par, cols, high, done):
                pool.wait_ge(high, k + 1)
                nc.gpsimd.tensor_tensor(w_lo[:, par, cols], w_raw[:, bass.ds(n, 1), cols].rearrange("p o c -> p (o c)"),
                                        w_hi[:, par, cols].bitcast(F32), ALU.subtract).then_inc(done, 1)

            def low_gu(k, n, par):
                low(k, n, par, slice(0, GU), hi_gu, lo_gu)

            def low_d(k, n, par):
                low(k, n, par, slice(GU, WCOL), hi_d, lo_d)

            def step(k, par, first):
                base = 0 if first + 2 < NF else NF
                if first + 2 < 2 * NF:
                    low_gu(k + 2, k + (2 - base), par)
                base = 0 if first + 1 < NF else NF
                if first + 1 < 2 * NF:
                    low_d(k + 1, k + (1 - base), 1 - par)

            for b in range(B):
                root(0, b)
            pool.wait_ge(gwhi_ready, 1)
            nc.gpsimd.tensor_tensor(gw_parts[:, :, E:2 * E], gw[:], gw_parts[:, :, 0:E].bitcast(F32), ALU.subtract)\
              .then_inc(gwlo_ready, 1)
            root(1, 0)
            root(1, 1)
            low_gu(0, 0, 0)
            pool.wait_ge(scaled_ready, 1)
            nc.gpsimd.tensor_tensor(x1[:, 3, :], prob[:, 3, :], xs[:, 3, :], ALU.add).then_inc(x1_ready[1], 1)
            root(2, 0)
            root(2, 1)
            low_d(0, 0, 0)
            low_gu(1, 1, 1)
            root(1, 2)
            each_step(pool, step, {2: [lambda: root(1, 3)], 8: [lambda: root(2, 2)], 10: [lambda: root(2, 3)]})

        @block.scalar
        def _(act):
            act.dma_start(cw[:], ctxw).then_inc(ctxw_in, 16)
            act.dma_start(vec[:], vecs.partition_broadcast(P).rearrange("p o v -> p (o v)")).then_inc(vec_in, 16)
            act.dma_start(gw[:], route_w.rearrange("(c p) e -> p c e", p=P)).then_inc(gw_in, 16)

            def high(n, par, cols, done):
                nc.scalar.copy(w_hi[:, par, cols], w_raw[:, bass.ds(n, 1), cols].rearrange("p o c -> p (o c)"))\
                  .then_inc(done, 1)

            def high_gu(k, n, par, landed, free=True):
                if landed is not None:
                    act.wait_ge(w_in[par], landed)
                if free:
                    act.wait_ge(up_done, k - 1)
                high(n, par, slice(0, GU), hi_gu)

            def high_d(k, n, par, free=True):
                if free:
                    act.wait_ge(down_done, k - 1)
                high(n, par, slice(GU, WCOL), hi_d)

            def kvT_copy(b):
                act.wait_ge(kvT_done, b + 1)
                nc.scalar.copy(kvT[:, b * S:(b + 1) * S], kvT_ps[0:CD, batch_cols(b)]).then_inc(kvT_ready, 1)

            def kv_copy(h):
                act.wait_ge(kv_done, h + 1)
                nc.scalar.copy(kv[:, HALF * h:HALF * h + HALF, :].rearrange("p t d -> p (t d)"),
                               kv_ps[:, 0:HALF * CD]).then_inc(kv_ready, 1)

            def ln_copy(b):
                act.wait_ge(lnT_done[b], 1)
                nc.scalar.copy(lnT[:, b, :, :].rearrange("p c t -> p (c t)"), lnT_ps[b][:, :])\
                  .then_inc(lnT_ready[b], 1)

            def q_copy(b):
                act.wait_ge(qT_done[b], 1)
                nc.scalar.copy(qT[:, b, :], qT_ps[b][0:CD, 0:S]).then_inc(qT_ready[b], 1)

            def softmax_exp(b):
                act.wait_ge(max_ready[b], 1)
                for t in tiles(b):
                    nc.scalar.activation(prob[:, t, :], logit[:, t, :], ACT.Exp, bias=neg_max[:, t:t + 1],
                                         accum_out=exp_sum[:, t:t + 1]).then_inc(exp_ready[b], 1)

            def hidden_high(b):
                act.wait_ge(hT_done[b], 1)
                nc.scalar.copy(hT_hi[:, b // 2, :, b % 2 * S:(b % 2 + 1) * S],
                               hT_ps[b][:, :].rearrange("p (c t) -> p c t", c=C)).then_inc(hThi_ready[b], 1)

            def logitT_copy(h):
                act.wait_ge(logitT_done, h + 1)
                nc.scalar.copy(logitT[:, h, :], logitT_ps[h][0:2 * E, :]).then_inc(logitT_ready, 1)

            def logit_exp(h):
                act.wait_ge(route_logit_ready, h + 1)
                nc.scalar.activation(inv_score[:, h, :, :], route_logit[:, h, :, :], ACT.Exp, scale=-1.0)\
                  .then_inc(score_ready, 1)

            def step(k, par, first):
                act.wait_ge(gate_done, k + 1)
                if first >= 2:
                    act.wait_ge(act_done, k - 1)
                nc.scalar.activation(silu_g[:, par, :], gate_ps[par][:, :], ACT.Silu).then_inc(silu_done, 1)
                if first in table_change:
                    table_change[first]()
                base = 0 if first + 2 < NF else NF
                if first + 2 < 2 * NF:
                    high_gu(k + 2, k + (2 - base), par, None if base else 8 * (k + (2 - par)) + 16)
                base = 0 if first + 1 < NF else NF
                if first + 1 < 2 * NF:
                    high_d(k + 1, k + (1 - base), 1 - par, first >= 1)

            def ffn_copy(b):
                act.wait_ge(down_done, summed(b))
                nc.scalar.copy(ffnT[:, b // 2, 0, batch_cols(b)], acc_ps[b // 2][0][:, batch_cols(b)])\
                  .then_inc(ffn0_ready, 1)

            table_change = {6: lambda: (softmax_exp(2), softmax_exp(3)), 15: lambda: logit_exp(1)}

            act.wait_ge(vec_in, 16)
            nc.scalar.activation(gates[:], vec[:, V_GATES:V_GATES + 2], ACT.Tanh).then_inc(gates_ready, 1)
            nc.scalar.activation(gamma_scaled[:], gamma, ACT.Copy, scale=SIM_SCALE).then_inc(gamma_ready, 1)
            act.wait_ge(gw_in, 16)
            nc.scalar.copy(gw_parts[:, :, 0:E], gw[:]).then_inc(gwhi_ready, 1)
            kv_copy(0)
            ln_copy(0)
            kvT_copy(0)
            q_copy(0)
            ln_copy(1)
            kvT_copy(1)
            q_copy(1)
            act.wait_ge(shift_ready, 1)
            for t in range(HALF, NT):
                nc.scalar.activation(ln[:, t, :], xs[:, t, :], ACT.Identity, scale=rstd[:, 0, t:t + 1],
                                     bias=shift[:, t - HALF:t - HALF + 1]).then_inc(ln_ready[t // 2], 1)
            kv_copy(1)
            high_gu(0, 0, 0, 16, False)
            kvT_copy(2)
            softmax_exp(0)
            ln_copy(2)
            kvT_copy(3)
            ln_copy(3)
            softmax_exp(1)
            q_copy(2)
            q_copy(3)
            act.wait_ge(scale_ready[1], 1)
            nc.scalar.activation(prob[:, 3, :], prob[:, 3, :], ACT.Copy, scale=attn_scale[:, 3:4])\
              .then_inc(scaled_ready, 1)
            high_d(0, 0, 0, False)
            high_gu(1, 1, 1, 16, False)
            hidden_high(0)
            hidden_high(1)
            logitT_copy(0)
            logit_exp(0)
            each_step(act, step, {
                12: [lambda: hidden_high(2), lambda: hidden_high(3)],
                13: [lambda: logitT_copy(1)],
                NF: [lambda: ffn_copy(0), lambda: ffn_copy(1)],
            })
            ffn_copy(2)
            ffn_copy(3)

        @block.vector
        def _(dve):
            order = [0]

            def mark(ins):
                order[0] += 1
                ins.then_inc(dve_order, 1)
                return order[0]

            def link(ins):
                dve.wait_ge(dve_order, mark(ins))

            def mean_var(layer, b, source, scale2, eps):
                marks = [mark(nc.vector.bn_stats(stats[:, layer, t, :], source(t))) for t in tiles(b)]
                for t, stats_done in zip(tiles(b), marks):
                    dve.wait_ge(dve_order, stats_done)
                    ins = nc.vector.bn_aggr(meanvar[:, layer, t, :], stats[:, layer, t, :])
                link(ins)
                ts = slice(2 * b, 2 * b + 2)
                nc.vector.tensor_scalar(var_eps[:, layer, ts], meanvar[:, layer, ts, 1], scale2, eps,
                                        ALU.mult, ALU.add).then_inc(var_ready, 1)

            def normalise(layer, b, n_root, source, dst, ready):
                dve.wait_ge(rstd_ready, n_root)
                for t in tiles(b):
                    nc.vector.tensor_scalar(dst[:, t, :], source[:, t, :], meanvar[:, layer, t, 0:1],
                                            rstd[:, layer, t:t + 1], ALU.subtract, ALU.mult).then_inc(ready[b], 1)

            def x_stats(b):
                dve.wait_ge(x_in[b], 16)
                mean_var(0, b, lambda t: xs[:, t, :], 1.0, LN_EPS)

            def sim_of(b, t):
                return sim_ps[b][:, (t % 2) * S:(t % 2 + 1) * S]

            def sim_stats(b):
                dve.wait_ge(sim_done[b], 1)
                mean_var(1, b, lambda t: sim_of(b, t), SIM_SCALE ** 2, SIM_EPS)

            def sim_centre(b):
                for t in tiles(b):
                    nc.vector.scalar_tensor_tensor(centred[:, t, :], sim_of(b, t), meanvar[:, 1, t, 0:1], gamma_scaled[:],
                                                   ALU.subtract, ALU.mult).then_inc(sim_read[b], 1)

            def sim_logits(b, n_root):
                dve.wait_ge(rstd_ready, n_root)
                dve.wait_ge(sim_read[b], 2)
                for t in tiles(b):
                    ins = nc.vector.scalar_tensor_tensor(logit[:, t, :], centred[:, t, :], rstd[:, 1, t:t + 1], beta,
                                                         ALU.mult, ALU.add)
                link(ins)
                ts = slice(2 * b, 2 * b + 2)
                nc.vector.tensor_reduce(neg_max[:, ts], logit[:, ts, :], AX.X, ALU.max, negate=True)\
                  .then_inc(max_ready[b], 1)

            def attention_scale(b):
                ts = slice(2 * b, 2 * b + 2)
                dve.wait_ge(exp_ready[b], 2)
                link(nc.vector.reciprocal(exp_rec[:, ts], exp_sum[:, ts]))
                nc.vector.tensor_scalar(attn_scale[:, ts], exp_rec[:, ts], gates[:, 0:1], None, ALU.mult)\
                  .then_inc(scale_ready[b], 1)

            def residual(b, ts=None):
                dve.wait_ge(scale_ready[b], 1)
                for t in ts or tiles(b):
                    nc.vector.scalar_tensor_tensor(x1[:, t, :], prob[:, t, :], attn_scale[:, t:t + 1], xs[:, t, :],
                                                   ALU.mult, ALU.add).then_inc(x1_ready[b], 1)

            def x1_stats(b):
                dve.wait_ge(x1_ready[b], 2)
                mean_var(2, b, lambda t: x1[:, t, :], 1.0, LN_EPS)

            def hidden_low(b):
                dve.wait_ge(hThi_ready[b], 1)
                cols = slice(b % 2 * S, (b % 2 + 1) * S)
                nc.vector.tensor_tensor(hT_lo[:, b // 2, :, cols], hT_ps[b][:, :].rearrange("p (c t) -> p c t", c=C),
                                        hT_hi[:, b // 2, :, cols].bitcast(F32), ALU.subtract)\
                  .then_inc(hTlo_ready[b], 1)

            def step(k, par, first):
                dve.wait_ge(silu_done, k + 1)
                gated = silu_g
                late = first in WEIGHTED_LAST
                if not late and not (first < NSH or NF <= first < NF + NSH):
                    routed = k + (1 - NSH if first < NF else 1 - 2 * NSH)
                    dve.wait_ge(row_in[par], 8 * (routed - (1 - par)))
                    nc.vector.tensor_tensor(weighted[:, par, :], silu_g[:, par, :], w_row[:, par, :], ALU.mult)\
                      .then_inc(weighted_done, 1)
                    dve.wait_ge(weighted_done, routed - len(WEIGHTED_LAST))
                    gated = weighted
                dve.wait_ge(up_done, k + 1)
                if first >= 2:
                    dve.wait_ge(actlo_done, k - 1)
                for toks in spans(first):
                    ins = nc.vector.tensor_tensor(act_f[:, par, toks], up_ps[par][:, toks], gated[:, par, toks],
                                                  ALU.mult)
                    if not late:
                        ins.then_inc(act_done, 1)
                if late:
                    link(ins)
                    if first == NSH:
                        dve.wait_ge(first_row_done, 1)
                        row = first_row_ps[:, :]
                    else:
                        dve.wait_ge(row_in[par], 16)
                        row = w_row[:, par, :]
                    ins = nc.vector.tensor_tensor(act_f[:, par, :], act_f[:, par, :], row, ALU.mult)
                    ins.then_inc(act_done, 1)
                if first >= 2:
                    dve.wait_ge(down_done, k - 1)
                for s, toks in enumerate(spans(first)):
                    dve.wait_ge(act_done, k + (s + 1))
                    nc.vector.tensor_copy(act_hi[:, par, toks], act_f[:, par, toks]).then_inc(acthi_done, 1)
                for s, toks in enumerate(spans(first)):
                    dve.wait_ge(acthi_done, k + (s + 1))
                    nc.vector.tensor_tensor(act_lo[:, par, toks], act_f[:, par, toks],
                                            act_hi[:, par, toks].bitcast(F32), ALU.subtract).then_inc(actlo_done, 1)

            member = choice[:].rearrange("p t (g m) -> p (t g) m", g=GROUPS)

            def add_logits(h):
                dve.wait_ge(logit_done, h + 1)
                both = logit_ps[h][:, 0:HALF * 2 * E].rearrange("p (t r e) -> p t e r", r=2, e=E)
                nc.vector.tensor_reduce(route_logit[:, h, :, :], both, AX.X, ALU.add).then_inc(route_logit_ready, 1)

            def score_groups(h):
                dve.wait_ge(score_ready, h + 1)
                bias = vec[:, V_BIAS:V_BIAS + E].unsqueeze(1).to_broadcast([P, HALF, E])
                link(nc.vector.tensor_scalar(inv_score[:, h], inv_score[:, h], 1.0, None, ALU.add))
                link(nc.vector.reciprocal(score[:, HALF * h:HALF * h + HALF, :], inv_score[:, h]))
                link(nc.vector.tensor_tensor(choice[:], score[:, HALF * h:HALF * h + HALF, :], bias, ALU.add))
                nc.vector.tensor_tensor(pairs[:, :, 0:3], member[:, :, 0:3], member[:, :, 1:4], ALU.add)
                nc.vector.tensor_tensor(pairs[:, :, 3:5], member[:, :, 0:2], member[:, :, 2:4], ALU.add)
                link(nc.vector.tensor_tensor(pairs[:, :, 5:6], member[:, :, 0:1], member[:, :, 3:4], ALU.add))
                link(nc.vector.tensor_reduce(gscore[:].rearrange("p t g -> p (t g)"), pairs[:], AX.X, ALU.max))

            def rank_groups():
                def grid(a):
                    return a.rearrange("p t (g h) -> p t g h", g=GROUPS)

                other = gscore[:].unsqueeze(2).to_broadcast([P, HALF, GROUPS, GROUPS])
                own = gscore[:].unsqueeze(3).to_broadcast([P, HALF, GROUPS, GROUPS])
                nc.vector.tensor_tensor(grid(beats[:]), other, own, ALU.is_gt)
                link(nc.vector.tensor_tensor(grid(ties[:]), other, own, ALU.is_equal))
                earlier = before[:].rearrange("p g h -> p (g h)").unsqueeze(1).to_broadcast([P, HALF, GROUPS * GROUPS])
                link(nc.vector.tensor_tensor(ties[:], ties[:], earlier, ALU.mult))
                link(nc.vector.tensor_tensor(beats[:], beats[:], ties[:], ALU.add))
                link(nc.vector.tensor_reduce(rank[:], beats[:].rearrange("p t (g h) -> p (t g) h", g=GROUPS),
                                             AX.X, ALU.add))

            def mask_groups():
                link(nc.vector.scalar_tensor_tensor(masked[:].rearrange("p t (g m) -> p (t g) m", g=GROUPS),
                                                    rank[:].unsqueeze(2).to_broadcast([P, HALF * GROUPS, E // GROUPS]),
                                                    -PEN, member, ALU.mult, ALU.min))
                for t in range(HALF):
                    ins = nc.vector.max(top8[:, t, :], masked[:, t, :])
                link(ins)
                link(nc.vector.memset(top8[:, :, TOPK:8], OUT_OF_GROUP))
                for t in range(HALF):
                    ins = nc.vector.match_replace(replaced[:, t, :], top8[:, t, :], masked[:, t, :], OUT_OF_GROUP)
                link(ins)

            def pick_experts(h):
                link(nc.vector.tensor_tensor(picked[:], masked[:], replaced[:], ALU.not_equal))
                link(nc.vector.tensor_tensor(pick_w[:], picked[:], score[:, HALF * h:HALF * h + HALF, :], ALU.mult))
                link(nc.vector.tensor_reduce(w_sum[:], pick_w[:], AX.X, ALU.add))
                link(nc.vector.tensor_scalar(w_sum[:], w_sum[:], 1.0 / ROUTED_SCALE, 1e-20 / ROUTED_SCALE,
                                             ALU.mult, ALU.add))
                link(nc.vector.reciprocal(w_rec[:], w_sum[:]))
                ins = nc.vector.tensor_tensor(w_tok[:, h, :, :].rearrange("p e t -> p t e"), pick_w[:],
                                              w_rec[:].unsqueeze(2).to_broadcast([P, HALF, E]), ALU.mult)
                ins.then_inc(weights_ready, 1)
                dve.wait_ge(weights_ready, h + 1)
                nc.vector.transpose(w_blk[:, h, :], w_tok[:, h, :, :].rearrange("p e t -> p (e t)"))\
                  .then_inc(blk_ready, 1)

            def ffn_copy(b):
                dve.wait_ge(down_done, summed(b))
                nc.vector.tensor_copy(ffnT[:, b // 2, 1, batch_cols(b)], acc_ps[b // 2][1][:, batch_cols(b)])\
                  .then_inc(ffn1_ready, 1)

            def result(b):
                dve.wait_ge(fin_done, b + 1)
                own = x1[:, 2 * b:2 * b + 2, :].rearrange("p t d -> p (t d)")
                nc.vector.scalar_tensor_tensor(own, fin_ps[b][:, :], gates[:, 1:2], own, ALU.mult, ALU.add)\
                  .then_inc(res_ready, 1)

            nc.vector.memset(zeros[:].bitcast(F32), 0.0).then_inc(zeros_ready, 1)
            x_stats(0)
            normalise(0, 0, 1, xs, ln, ln_ready)
            x_stats(1)
            normalise(0, 1, 2, xs, ln, ln_ready)
            x_stats(2)
            x_stats(3)
            dve.wait_ge(gamma_ready, 1)
            sim_stats(0)
            dve.wait_ge(rstd_ready, 4)
            nc.vector.scalar_tensor_tensor(shift[:], meanvar[:, 0, HALF:NT, 0], -1.0, rstd[:, 0, HALF:NT],
                                           ALU.mult, ALU.mult).then_inc(shift_ready, 1)
            sim_centre(0)
            sim_logits(0, 5)
            sim_stats(1)
            sim_centre(1)
            sim_logits(1, 6)
            dve.wait_ge(gates_ready, 1)
            attention_scale(0)
            residual(0)
            attention_scale(1)
            x1_stats(0)
            residual(1, (2,))
            x1_stats(1)
            normalise(2, 0, 7, x1, hid, hid_ready)
            normalise(2, 1, 8, x1, hid, hid_ready)
            hidden_low(0)
            hidden_low(1)
            sim_stats(2)
            sim_centre(2)
            dve.wait_ge(consts_ready, 2 + 2 * GROUPS - 1)
            add_logits(0)
            score_groups(0)
            each_step(dve, step, {
                0: [rank_groups, mask_groups],
                1: [lambda: pick_experts(0)],
                2: [lambda: sim_stats(3), lambda: sim_centre(3)],
                4: [lambda: sim_logits(2, 9)],
                5: [lambda: sim_logits(3, 10)],
                7: [lambda: attention_scale(2), lambda: residual(2)],
                8: [lambda: x1_stats(2)],
                9: [lambda: attention_scale(3), lambda: residual(3)],
                10: [lambda: x1_stats(3)],
                11: [lambda: normalise(2, 2, 11, x1, hid, hid_ready), lambda: normalise(2, 3, 12, x1, hid, hid_ready)],
                12: [lambda: hidden_low(2), lambda: hidden_low(3)],
                14: [lambda: add_logits(1)],
                15: [lambda: score_groups(1), rank_groups],
                16: [mask_groups],
                17: [lambda: pick_experts(1)],
                NF: [lambda: ffn_copy(0), lambda: ffn_copy(1)],
                NF + 1: [lambda: result(0), lambda: result(1)],
            })
            ffn_copy(2)
            ffn_copy(3)
            result(2)
            result(3)

        @block.tensor
        def _(pe):
            wk = cw[:, B * S:B * S + CD]

            def project(h):
                for t in range(HALF):
                    positions = slice((HALF * h + t) * P, (HALF * h + t + 1) * P)
                    last = nc.tensor.matmul(kv_ps[:, t * CD:(t + 1) * CD], cw[:, positions], wk,
                                            start=True, stop=True)
                last.then_inc(kv_done, 1)

            def project_transposed(b):
                nc.tensor.matmul(kvT_ps[0:CD, batch_cols(b)], wk, cw[:, b * S:(b + 1) * S], start=True, stop=True)\
                  .then_inc(kvT_done, 1)

            def transposes(b, dst, source, ready, done):
                for i, t in enumerate(tiles(b)):
                    pe.wait_ge(ready[b], i + 1)
                    for c in range(C):
                        last = nc.tensor.transpose(dst[b][:, c * S + i * P:c * S + (i + 1) * P],
                                                   source[:, t, c * P:(c + 1) * P], ident[:])
                last.then_inc(done[b], 1)

            def query(b):
                pe.wait_ge(lnT_ready[b], 1)
                pe.wait_ge(kv_ready, b // 2 + 1)
                for c in range(C):
                    last = nc.tensor.matmul(qT_ps[b][0:CD, 0:S], kv[:, 2 * b + c, :], lnT[:, b, c, :],
                                            start=(c == 0), stop=(c == C - 1))
                last.then_inc(qT_done[b], 1)

            def similarity(b):
                pe.wait_ge(qT_ready[b], 1)
                pe.wait_ge(kvT_ready, b + 1)
                for i in range(2):
                    last = nc.tensor.matmul(sim_ps[b][:, i * S:(i + 1) * S], qT[:, b, i * P:(i + 1) * P],
                                            kvT[:, b * S:(b + 1) * S], start=True, stop=True)
                last.then_inc(sim_done[b], 1)

            def hidden(b):
                pe.wait_ge(sim_read[b], 2)
                transposes(b, hT_ps, hid, hid_ready, hT_done)

            def route(h):
                for b in (2 * h, 2 * h + 1):
                    pe.wait_ge(hThi_ready[b], 1)
                pe.wait_ge(gwlo_ready, 1)
                pe.wait_ge(kv_ready, 2)
                pe.wait_ge(kvT_ready, B)
                if h == 1:
                    pe.wait_ge(hTlo_ready[2], 1)
                    pe.wait_ge(hTlo_ready[3], 1)
                moving = [(c, m) for m in (hT_hi, hT_lo) for c in range(C)]
                for i, (c, m) in enumerate(moving):
                    if i == C:
                        for b in (2 * h, 2 * h + 1):
                            pe.wait_ge(hTlo_ready[b], 1)
                    last = nc.tensor.matmul(logitT_ps[h][0:2 * E, :], gw_parts[:, c, :], m[:, h, c, :],
                                            start=(i == 0), stop=(i == len(moving) - 1))
                last.then_inc(logitT_done, 1)

            def route_back(h):
                pe.wait_ge(logitT_ready, h + 1)
                for t in range(HALF):
                    last = nc.tensor.transpose(logit_ps[h][:, t * 2 * E:(t + 1) * 2 * E],
                                               logitT[:, h, t * P:(t + 1) * P], ident[0:2 * E, 0:2 * E])
                last.then_inc(logit_done, 1)

            def first_row():
                pe.wait_ge(weights_ready, 1)
                pe.wait_ge(sim_read[2], 2)
                for t in range(HALF):
                    last = nc.tensor.transpose(first_row_ps[:, t * P:(t + 1) * P],
                                               w_tok[:, 0, 0, t:t + 1].to_broadcast([P, P]), ident[:])
                last.then_inc(first_row_done, 1)

            def product(k, dst, w0, moving, par, midway=None):
                parts = [(w_hi, c, m) for c in range(C) for m in moving[c]]
                parts += [(w_lo, c, moving[c][0]) for c in range(C)]
                for i, (w, c, m) in enumerate(parts):
                    if midway is not None and i == len(parts) // 2:
                        midway()
                    if w is w_lo:
                        pe.wait_ge(lo_gu, k + 1)
                    last = nc.tensor.matmul(dst, w[:, par, w0 + c * P:w0 + (c + 1) * P], m, start=i == 0,
                                            stop=i == len(parts) - 1, skip_group_check=True)
                return last

            def first_gate(b):
                pe.wait_ge(hi_gu, 1)
                pe.wait_ge(lo_gu, 1)
                pe.wait_ge(hThi_ready[b], 1)
                for i, (w, m) in enumerate(((w_hi, hT_hi), (w_lo, hT_hi), (w_hi, hT_lo))):
                    if m is hT_lo:
                        pe.wait_ge(hTlo_ready[b], 1)
                    for c in range(C):
                        last = nc.tensor.matmul(gate_ps[0][:, batch_cols(b)], w[:, 0, c * P:(c + 1) * P],
                                                m[:, 0, c, batch_cols(b)], start=i == c == 0,
                                                stop=i == 2 and c == C - 1, skip_group_check=True)
                return last

            def gate_up(k, par, half, first):
                pe.wait_ge(hi_gu, k + 1)
                moving = [(hT_hi[:, half, c, :], hT_lo[:, half, c, :]) for c in range(C)]
                if first >= 2:
                    pe.wait_ge(silu_done, k - 1)
                if first == 0:
                    first_gate(1).then_inc(gate_done, 1)
                    route_back(0)
                else:
                    midway = first_row if first == NSH + 1 else None
                    product(k, gate_ps[par][:, :], 0, moving, par, midway).then_inc(gate_done, 1)
                if first >= 2:
                    pe.wait_ge(act_done, k - 1)
                product(k, up_ps[par][:, :], C * P, moving, par).then_inc(up_done, 1)

            def down(k, par, half, start, token_spans=spans(0)):
                pe.wait_ge(hi_d, k + 1)
                pe.wait_ge(lo_d, k + 1)
                for s, toks in enumerate(token_spans):
                    pe.wait_ge(acthi_done, k + (s + 1))
                    for i, (w, m) in enumerate(((w_hi, act_hi), (w_lo, act_hi), (w_hi, act_lo))):
                        if m is act_lo:
                            pe.wait_ge(actlo_done, k + (s + 1))
                        for c in range(C):
                            cols = slice(GU + c * P, GU + (c + 1) * P)
                            last = nc.tensor.matmul(acc_ps[half][c][:, toks], w[:, par, cols], m[:, par, toks],
                                                    start=start and i == 0, stop=i == 2, skip_group_check=True)
                    last.then_inc(down_done, 1)

            def step(k, par, first):
                gate_up(k, par, int(first >= NF), first)
                if first == 1:
                    pe.wait_ge(score_ready, 1)
                if first == NF + 1:
                    pe.wait_ge(score_ready, 2)
                if first >= 1:
                    down(k - 1, 1 - par, int(first - 1 >= NF), first - 1 in (0, NF))

            def finish(b):
                copied = 2 if b < 2 else b + 1
                pe.wait_ge(ffn0_ready, copied)
                pe.wait_ge(ffn1_ready, copied)
                if b >= 2:
                    pe.wait_ge(silu_done, 2 * NF - 3 + b)
                for i in range(2):
                    for c in range(C):
                        tok = slice((b % 2 * 2 + i) * P, (b % 2 * 2 + i + 1) * P)
                        last = nc.tensor.transpose(fin_ps[b][:, i * D + c * P:i * D + (c + 1) * P],
                                                   ffnT[:, b // 2, c, tok], ident[:])
                last.then_inc(fin_done, 1)

            def keep_warm(n):
                for i in range(n):
                    last = nc.tensor.matmul(bank[5][:, :], zeros[:, 0:P], zeros[:], start=True, stop=True)
                last.then_inc(warm_done, 1)

            pe.wait_ge(ctxw_in, 16)
            project(0)
            pe.wait_ge(ident_ready, 2)
            transposes(0, lnT_ps, ln, ln_ready, lnT_done)
            project_transposed(0)
            query(0)
            transposes(1, lnT_ps, ln, ln_ready, lnT_done)
            similarity(0)
            pe.wait_ge(kvT_ready, 1)
            project_transposed(1)
            query(1)
            similarity(1)
            pe.wait_ge(kv_ready, 1)
            project(1)
            for b in (2, 3):
                pe.wait_ge(kvT_ready, b)
                project_transposed(b)
                transposes(b, lnT_ps, ln, ln_ready, lnT_done)
            for b in (2, 3):
                query(b)
            for b in (2, 3):
                similarity(b)
            pe.wait_ge(zeros_ready, 1)
            keep_warm(6)
            hidden(0)
            hidden(1)
            first_gate(0)
            route(0)
            each_step(pe, step, {
                12: [lambda: hidden(2), lambda: hidden(3)],
                13: [lambda: route(1)],
                14: [lambda: route_back(1)],
                NF + 1: [lambda: finish(0), lambda: finish(1)],
            })
            down(2 * NF - 1, 1, 1, False, spans(2 * NF - 1))
            finish(2)
            finish(3)


def kernel(x, ctx_512, g_xattn, g_ffn, L0_xattn_W_k, L0_xattn_b_k, L0_xattn_ln_gamma, L0_xattn_ln_beta,
           L0_ffn_gate_weight, L0_ffn_e_score_correction_bias, L0_ffn_gate_w, L0_ffn_up_w, L0_ffn_down_w,
           L0_ffn_sh_gate_w, L0_ffn_sh_up_w, L0_ffn_sh_down_w):
    import numpy as np
    import concourse.bacc as bacc
    from concourse.bass_utils import run_bass_kernel_spmd as run

    def arr(a):
        return np.asarray(a)

    def slices(gate, up, down):
        n = gate.shape[0]
        parts = [w.transpose(0, 2, 1).reshape(n, C, P, P).transpose(0, 2, 1, 3).reshape(n, P, C * P)
                 for w in (gate, up)]
        return np.concatenate(parts + [down.transpose(0, 2, 1)], axis=2)

    tokens = B * S
    ctxT = arr(ctx_512).reshape(tokens, CD).T
    ones = np.ones((1, tokens), np.float32)
    wk = np.concatenate([arr(L0_xattn_W_k).T, arr(L0_xattn_b_k).reshape(1, CD)], axis=0)
    sh = slices(arr(L0_ffn_sh_gate_w).reshape(NSH, P, D), arr(L0_ffn_sh_up_w).reshape(NSH, P, D),
                arr(L0_ffn_sh_down_w).reshape(D, NSH, P).transpose(1, 0, 2))
    arrays = {
        "x_in": arr(x).reshape(tokens, D),
        "ctxw_in": np.concatenate([np.concatenate([ctxT, ones], axis=0), wk], axis=1),
        "vecs_in": np.concatenate([arr(a).reshape(-1) for a in (
            L0_xattn_ln_gamma, L0_xattn_ln_beta, L0_ffn_e_score_correction_bias, g_xattn, g_ffn)]).reshape(1, -1),
        "route_in": arr(L0_ffn_gate_weight).T,
        "w_in": np.concatenate([sh, slices(arr(L0_ffn_gate_w), arr(L0_ffn_up_w), arr(L0_ffn_down_w))], axis=0),
    }
    arrays = {k: np.ascontiguousarray(v) for k, v in arrays.items()}
    nc = bacc.Bacc("TRN2", target_bir_lowering=False, num_devices=1)
    args = [nc.dram_tensor(k, v.shape, F32, kind="ExternalInput").ap() for k, v in arrays.items()]
    out = nc.dram_tensor("out", (tokens, D), F32, kind="ExternalOutput").ap()
    build(nc, *args, out)
    r = run(nc, [arrays], core_ids=[0])
    return r.results[0]["out"].reshape(B, S, D)
```
